# Optimizing a Trainium2 kernel written in Bass

```python
import numpy as np
import jax
import jax.numpy as jnp

def _softmax(x, axis=-1):
    return jax.nn.softmax(x, axis=axis)

def _gelu(x):
    return jax.nn.gelu(x, approximate=True)

def _silu(x):
    return jax.nn.silu(x)

def _sigmoid(x):
    return jax.nn.sigmoid(x)

def _layernorm(x, axis=-1, eps=1e-05):
    m = jnp.mean(x, axis=axis, keepdims=True)
    v = jnp.var(x, axis=axis, keepdims=True)
    return (x - m) / jnp.sqrt(v + eps)

def _scatter_add(tgt, idx, src, axis=0):
    return tgt.at[idx].add(src)

def _segment_sum(src, seg, n):
    return jax.ops.segment_sum(src, seg, n)
kernel_name = 'mk_seq_postln_d1_jaxref_r8_55fa6e'

def setup_inputs(seed: int=0):
    np.random.seed(seed)
    _w = jnp.asarray

    def _L0_attn_setup():
        import jax, jax.numpy as jnp
        import numpy as np
        import math
        D_MODEL, N_HEADS, D_K, D_C, D_HR = (128, 8, 128, 32, 32)
        B, S = (4, 256)
        key = jax.random.key(seed)
        ks = jax.random.split(key, 17)

        def lin(k, fan_in, fan_out):
            lim = 1.0 / math.sqrt(fan_in)
            kw, kb = jax.random.split(k)
            W = jax.random.uniform(kw, (fan_in, fan_out), jnp.float32, -lim, lim)
            b = jax.random.uniform(kb, (fan_out,), jnp.float32, -lim, lim)
            return (W, b)
        W_DQ, b_DQ = lin(ks[0], D_MODEL, D_C)
        W_UQ, b_UQ = lin(ks[1], D_C, N_HEADS * D_K)
        W_DKV, b_DKV = lin(ks[2], D_MODEL, D_C)
        W_UK, b_UK = lin(ks[3], D_C, N_HEADS * D_K)
        W_UV, b_UV = lin(ks[4], D_C, N_HEADS * D_K)
        W_QR, b_QR = lin(ks[5], D_C, N_HEADS * D_HR)
        W_KR, b_KR = lin(ks[6], D_MODEL, D_HR)
        W_O, b_O = lin(ks[7], N_HEADS * D_K, D_MODEL)
        h_t = jax.random.normal(ks[8], (B, S, D_MODEL), jnp.float32)
        return {'h_t': h_t, 'W_DQ': W_DQ, 'b_DQ': b_DQ, 'W_UQ': W_UQ, 'b_UQ': b_UQ, 'W_DKV': W_DKV, 'b_DKV': b_DKV, 'W_UK': W_UK, 'b_UK': b_UK, 'W_UV': W_UV, 'b_UV': b_UV, 'W_QR': W_QR, 'b_QR': b_QR, 'W_KR': W_KR, 'b_KR': b_KR, 'W_O': W_O, 'b_O': b_O}
    _L0_attn_in = _L0_attn_setup()

    def _L0_ffn_setup():
        import jax, jax.numpy as jnp
        import numpy as np
        DIM = 128
        HIDDEN = 384
        SCALE = 1.0 / 127.0

        def _dequant(w_int, dtype):
            return w_int.astype(dtype) * jnp.asarray(SCALE, dtype)
        key = jax.random.key(seed)
        k_x, k_g, k_u, k_d = jax.random.split(key, 4)
        x = jax.random.normal(k_x, (4, 256, DIM), dtype=jnp.float32)
        w_gate = jax.random.randint(k_g, (HIDDEN, DIM), -127, 128, dtype=jnp.int32)
        w_up = jax.random.randint(k_u, (HIDDEN, DIM), -127, 128, dtype=jnp.int32)
        w_down = jax.random.randint(k_d, (DIM, HIDDEN), -127, 128, dtype=jnp.int32)
        return {'x': x, 'w_gate': w_gate, 'w_up': w_up, 'w_down': w_down}
    _L0_ffn_in = _L0_ffn_setup()
    _d = {'L0_attn_h_t': _L0_attn_in['h_t'], 'L0_attn_W_DQ': _L0_attn_in['W_DQ'], 'L0_attn_b_DQ': _L0_attn_in['b_DQ'], 'L0_attn_W_UQ': _L0_attn_in['W_UQ'], 'L0_attn_b_UQ': _L0_attn_in['b_UQ'], 'L0_attn_W_DKV': _L0_attn_in['W_DKV'], 'L0_attn_b_DKV': _L0_attn_in['b_DKV'], 'L0_attn_W_UK': _L0_attn_in['W_UK'], 'L0_attn_b_UK': _L0_attn_in['b_UK'], 'L0_attn_W_UV': _L0_attn_in['W_UV'], 'L0_attn_b_UV': _L0_attn_in['b_UV'], 'L0_attn_W_QR': _L0_attn_in['W_QR'], 'L0_attn_b_QR': _L0_attn_in['b_QR'], 'L0_attn_W_KR': _L0_attn_in['W_KR'], 'L0_attn_b_KR': _L0_attn_in['b_KR'], 'L0_attn_W_O': _L0_attn_in['W_O'], 'L0_attn_b_O': _L0_attn_in['b_O'], 'L0_ffn_w_gate': _L0_ffn_in['w_gate'], 'L0_ffn_w_up': _L0_ffn_in['w_up'], 'L0_ffn_w_down': _L0_ffn_in['w_down']}
    _x0 = _d['L0_attn_h_t']
    _d['L0_attn_h_t'] = jax.random.normal(jax.random.fold_in(jax.random.key(seed), 1), (1, 2048, 128), dtype=_x0.dtype)
    del _x0
    return _d

def reference(L0_attn_h_t, L0_attn_W_DQ, L0_attn_b_DQ, L0_attn_W_UQ, L0_attn_b_UQ, L0_attn_W_DKV, L0_attn_b_DKV, L0_attn_W_UK, L0_attn_b_UK, L0_attn_W_UV, L0_attn_b_UV, L0_attn_W_QR, L0_attn_b_QR, L0_attn_W_KR, L0_attn_b_KR, L0_attn_W_O, L0_attn_b_O, L0_ffn_w_gate, L0_ffn_w_up, L0_ffn_w_down):

    def _L0_attn_ref(h_t, W_DQ, b_DQ, W_UQ, b_UQ, W_DKV, b_DKV, W_UK, b_UK, W_UV, b_UV, W_QR, b_QR, W_KR, b_KR, W_O, b_O):
        import jax, jax.numpy as jnp
        import numpy as np
        import math
        D_MODEL, N_HEADS, D_K, D_C, D_HR = (128, 8, 128, 32, 32)
        B, S = (4, 256)
        b, s, _ = h_t.shape
        c_q = h_t @ W_DQ + b_DQ
        c_kv = h_t @ W_DKV + b_DKV
        q_c = (c_q @ W_UQ + b_UQ).reshape(b, s, N_HEADS, D_K).transpose(0, 2, 1, 3)
        k_c = (c_kv @ W_UK + b_UK).reshape(b, s, N_HEADS, D_K).transpose(0, 2, 1, 3)
        v_c = (c_kv @ W_UV + b_UV).reshape(b, s, N_HEADS, D_K).transpose(0, 2, 1, 3)
        q_r = (c_q @ W_QR + b_QR).reshape(b, s, N_HEADS, D_HR).transpose(0, 2, 1, 3)
        k_r = (h_t @ W_KR + b_KR)[:, None, :, :]
        k_r = jnp.broadcast_to(k_r, (b, N_HEADS, s, D_HR))
        q = jnp.concatenate([q_c, q_r], axis=-1)
        k = jnp.concatenate([k_c, k_r], axis=-1)
        scale = 1.0 / math.sqrt(D_K + D_HR)
        scores = jnp.einsum('bhsd,bhtd->bhst', q, k) * scale
        attn = jax.nn.softmax(scores, axis=-1)
        o = jnp.einsum('bhst,bhtd->bhsd', attn, v_c)
        o = o.transpose(0, 2, 1, 3).reshape(b, s, N_HEADS * D_K)
        return o @ W_O + b_O

    def _L0_ffn_ref(x, w_gate, w_up, w_down):
        import jax, jax.numpy as jnp
        import numpy as np
        DIM = 128
        HIDDEN = 384
        SCALE = 1.0 / 127.0

        def _dequant(w_int, dtype):
            return w_int.astype(dtype) * jnp.asarray(SCALE, dtype)
        wg = _dequant(w_gate, x.dtype)
        wu = _dequant(w_up, x.dtype)
        wd = _dequant(w_down, x.dtype)
        gate = jnp.einsum('bsd,hd->bsh', x, wg)
        up = jnp.einsum('bsd,hd->bsh', x, wu)
        h = jax.nn.silu(gate) * up
        return jnp.einsum('bsh,dh->bsd', h, wd)
    x = L0_attn_h_t
    x = _layernorm(x + _L0_attn_ref(x, L0_attn_W_DQ, L0_attn_b_DQ, L0_attn_W_UQ, L0_attn_b_UQ, L0_attn_W_DKV, L0_attn_b_DKV, L0_attn_W_UK, L0_attn_b_UK, L0_attn_W_UV, L0_attn_b_UV, L0_attn_W_QR, L0_attn_b_QR, L0_attn_W_KR, L0_attn_b_KR, L0_attn_W_O, L0_attn_b_O), axis=-1)
    x = _layernorm(x + _L0_ffn_ref(x, L0_ffn_w_gate, L0_ffn_w_up, L0_ffn_w_down), axis=-1)
    return x

_drawn_inputs = setup_inputs


def setup_inputs(seed=0):
    import zlib

    import numpy as np

    out = dict(_drawn_inputs(seed))
    spreads = {}
    factors = {'L0_attn_W_DQ': 8.0,
     'L0_attn_b_DQ': 8.0,
     'L0_attn_W_UQ': 8.0,
     'L0_attn_b_UQ': 8.0,
     'L0_attn_W_DKV': 8.0,
     'L0_attn_b_DKV': 2.981,
     'L0_attn_W_UK': 8.0,
     'L0_attn_b_UK': 64.0,
     'L0_attn_W_QR': 8.0,
     'L0_attn_b_QR': 8.0,
     'L0_attn_W_KR': 8.0,
     'L0_attn_b_KR': 64.0,
     'L0_attn_b_O': 4.326}
    for name, (base, spread) in spreads.items():
        noise = np.random.default_rng([zlib.crc32(name.encode()), seed]).standard_normal(out[name].shape)
        drawn = base * np.exp(spread * noise) if base else spread * noise
        out[name] = jnp.asarray(drawn.astype(out[name].dtype))
    for name, factor in factors.items():
        out[name] = (out[name] * factor).astype(out[name].dtype)
    return out
```

```python
import numpy as np
import concourse.bass as bass
from concourse import mybir
from contextlib import ExitStack

F32 = mybir.dt.float32
F32R = mybir.dt.float32r
I32 = mybir.dt.int32
ALU = mybir.AluOpType
ACT = mybir.ActivationFunctionType
AX = mybir.AxisListType


def attention_ffn(nc, x, xT, wdq4, wk4, wdkv, bdq4, bk4, bdkv, uq4, ukb, buq, wqr, bqr,
                  uvT2, wo, bo, wg, wu, wd, out):
    P = 128
    S = x.shape[0]
    D = x.shape[1]
    HEADS = uq4.shape[1]
    R = wdkv.shape[1]
    FEAT = 2 * R
    QB = 512
    NJ = S // QB
    NB = HEADS * NJ
    QT = QB // P
    KT = S // P
    STEPS = KT // 2
    HALF = S // 2
    UNITS = 2 * QT
    AHEAD = UNITS + 3
    VC = 2 * R + 1
    DEN = D
    H = wg.shape[1]
    HT = H // P
    SCALE = 1.0 / float(np.sqrt(P + R))
    WSCALE = float(np.float32(1.0 / 127.0))
    EPS = 1e-5
    assert UNITS == STEPS and D == P and x.shape[1] == P

    ctx = ExitStack()
    with ctx:
        def sb(name, shape, dt=F32):
            return ctx.enter_context(nc.sbuf_tensor(name, shape, dt))

        def ps(name, shape):
            return ctx.enter_context(nc.psum_tensor(name, shape, F32))

        def sem(name):
            return ctx.enter_context(nc.semaphore(name))

        xT_sb = sb("xT_sb", [P, S])
        resid = sb("resid", [P, KT, D])
        bo_sb = sb("bo_sb", [P, D])
        wdq4_sb = sb("wdq4_sb", [P, 4 * R])
        wk4_sb = sb("wk4_sb", [P, 4 * R])
        wdkv_sb = sb("wdkv_sb", [P, R])
        bdq4_sb = sb("bdq4_sb", [P, 1])
        bk4_sb = sb("bk4_sb", [P, 1])
        bdkv_sb = sb("bdkv_sb", [1, R])
        uq4_sb = sb("uq4_sb", [P, HEADS, 4 * R])
        ukb_sb = sb("ukb_sb", [P, HEADS, R + 1])
        buq_sb = sb("buq_sb", [P, HEADS])
        uvT2_sb = sb("uvT2_sb", [P, HEADS, VC])
        wo_sb = sb("wo_sb", [P, HEADS, D])
        wint = sb("wint", [P, 2 * H + HT * D], I32)
        wffn = sb("wffn", [P, 2 * H + HT * D])

        ident = sb("ident", [P, P])
        ident_r = sb("ident_r", [P, P], F32R)
        ones_row = sb("ones_row", [1, P])
        eps_col = sb("eps_col", [P, 1])

        kf = sb("kf", [P, S])
        k_hi2 = sb("k_hi2", [P, S], F32R)
        k_lo2 = sb("k_lo2", [P, S], F32R)
        k_lo1 = sb("k_lo1", [FEAT + 2, S], F32R)
        cqf = sb("cqf", [P, S])
        cq_hl = sb("cq_hl", [P, S], F32R)
        vf = sb("vf", [P, KT, R])
        vals = sb("vals", [P, KT, VC], F32R)
        wqf = sb("wqf", [P, HEADS, FEAT])
        wq = sb("wq", [P, HEADS, 2 * FEAT], F32R)
        wq_now = sb("wq_now", [P, 2 * FEAT], F32R)
        qb_now = sb("qb_now", [P, 1])
        qbias = sb("qbias", [P, HEADS])
        uwf = sb("uwf", [P, HEADS])
        uw = sb("uw", [P, HEADS], F32R)
        uconst = sb("uconst", [P, HEADS])
        u = sb("u", [P, HEADS * KT])
        wvo = sb("wvo", [VC, HEADS, D + 1])

        q_hl = [sb(f"q_hl{j}", [P, QB], F32R) for j in range(NJ)]
        q_hm = [sb(f"q_hm{j}", [FEAT + 2, QB], F32R) for j in range(NJ)]
        mx_part = [sb(f"mx_part{j}", [P, QT, 2]) for j in range(2)]
        mx = sb("mx", [P, QT])
        mxu = sb("mxu", [P, QT])
        shift = sb("shift", [P, QT])
        shift_hl = sb("shift_hl", [P, QT, 2], F32R)
        NPH = 4
        p_hi = [sb(f"p_hi{n}", [P, 2 * QB], F32R) for n in range(NPH)]
        p_lo = [sb(f"p_lo{n}", [P, 2 * QB], F32R) for n in range(NPH)]
        p_f = [sb(f"p_f{n}", [P, 2 * QB]) for n in range(2)]
        ctx_sb = sb("ctx_sb", [VC, QB])
        rden = sb("rden", [P, QT])

        score = [ps(f"score{n}", [P, 2 * QB]) for n in range(2)]
        mscore = ps("mscore", [P, HALF])
        ctx_ps = ps("ctx_ps", [P, QB])
        misc = ps("misc", [P, QB])
        outp = misc[:, :].rearrange("p (t c) -> p t c", t=2)

        stats = sb("stats", [P, KT, 6])
        mv = sb("mv", [P, KT, 2])
        std = sb("std", [P, KT])
        rstd = sb("rstd", [P, KT])
        x1T = kf
        hT = sb("hT", [P, HT, QB])
        sil = sb("sil", [P, HT, QB])

        in_k = sem("in_k")
        in_q = sem("in_q")
        in_v = sem("in_v")
        in_x = sem("in_x")
        in_f = sem("in_f")
        const = sem("const")
        ident_ok = sem("ident_ok")
        pe_k = sem("pe_k")
        act_k = sem("act_k")
        dve_k = sem("dve_k")
        pool_k = sem("pool_k")
        pe_c = sem("pe_c")
        act_c = sem("act_c")
        dve_c = sem("dve_c")
        pe_w = sem("pe_w")
        act_w = sem("act_w")
        dve_w = sem("dve_w")
        wq_ok = sem("wq_ok")
        proj_ok = sem("proj_ok")
        qhi_ok = sem("qhi_ok")
        qlo_ok = sem("qlo_ok")
        unit_ok = sem("unit_ok")
        unit_max = sem("unit_max")
        mchain = sem("mchain")
        shift_ok = sem("shift_ok")
        row_ok = sem("row_ok")
        row_in = sem("row_in")
        score_ok = sem("score_ok")
        phi_ok = sem("phi_ok")
        pf_ok = sem("pf_ok")
        plo_ok = sem("plo_ok")
        pv_ok = sem("pv_ok")
        ctx_ok = sem("ctx_ok")
        outp_ok = sem("outp_ok")
        den_ok = sem("den_ok")
        added = sem("added")
        ffw_ok = sem("ffw_ok")
        ln = sem("ln")
        std_ok = sem("std_ok")
        x1T_ps = sem("x1T_ps")
        x1T_ok = sem("x1T_ok")
        gate_ok = sem("gate_ok")
        sil_ok = sem("sil_ok")
        h_ok = sem("h_ok")
        down_ok = sem("down_ok")
        y_ok = sem("y_ok")
        out_ok = sem("out_ok")

        block = ctx.enter_context(nc.Block())
        resid_v = x.rearrange("(t p) d -> p t d", p=P)
        out_v = out.rearrange("(t p) d -> p t d", p=P)

        def chunk(c):
            return slice(c * QB, (c + 1) * QB)

        def blocks(eng, body):
            body(0, 0)
            with eng.Fori(0, HEADS - 1) as t:
                for c in range(1, NJ + 1):
                    body(t, c)
            for c in range(NB - NJ + 1, NB):
                body(HEADS - 1, c - NB + NJ)

        def is_block(t, c):
            return not isinstance(t, int) or 0 <= NJ * t + c < NB

        def nth(t, c):
            return t * NJ + c

        def nstep(t, c, s):
            return t * (NJ * STEPS) + (c * STEPS + s)

        def head_of(t, c):
            return t + c // NJ

        def gate_t(k):
            return (score[0][:, 0:QB], score[0][:, QB:2 * QB], score[1][:, 0:QB])[k]

        def up_t(k):
            return (score[1][:, QB:2 * QB], mscore[:, 0:QB], mscore[:, QB:2 * QB])[k]

        CONST_ALL = 8

        LN_VAR = 2 * KT
        LN_ALL = LN_VAR + 1 + KT

        def ctx_misc(j):
            return (misc, ctx_ps)[j % 2][:, :]

        @block.sync
        def _(sp):
            for t, d in ((wk4_sb[:, :], wk4), (bk4_sb[:, :], bk4), (wdq4_sb[:, :], wdq4), (bdq4_sb[:, :], bdq4)):
                sp.dma_start(t, d).then_inc(in_k, 16)
            for c in range(NJ):
                sp.dma_start(xT_sb[:, chunk(c)], xT[:, chunk(c)]).then_inc(in_k, 16)
            for t, d in ((wdkv_sb[:, :], wdkv), (bdkv_sb[:, :], bdkv), (uvT2_sb[:, :, :], uvT2), (wo_sb[:, :, :], wo)):
                sp.dma_start(t, d).then_inc(in_v, 16)
            sp.dma_start(resid[:, :, :], resid_v).then_inc(in_x, 16)
            sp.dma_start(bo_sb[:, :], bo.partition_broadcast(P)).then_inc(in_x, 16)
            for t, d in ((wint[:, 0:H], wg), (wint[:, H:2 * H], wu),
                         (wint[:, 2 * H:2 * H + HT * D].rearrange("p (k d) -> p k d", k=HT), wd)):
                sp.dma_start(t, d).then_inc(in_f, 16)
            for j in range(NJ):
                sp.wait_ge(ln, LN_ALL + LN_VAR + 1 + (j + 1) * QT)
                sp.dma_start(out_v[:, j * QT:(j + 1) * QT, :], resid[:, j * QT:(j + 1) * QT, :]).then_inc(out_ok, 16)
            sp.wait_ge(out_ok, 16 * NJ)

        @block.gpsimd
        def _(pool):
            nc.gpsimd.memset(ident[:, :], 0.0).then_inc(const, 1)
            nc.gpsimd.memset(eps_col[:, :], EPS).then_inc(const, 1)
            nc.gpsimd.memset(vals[:, :, 2 * R:VC].bitcast(F32), 1.0).then_inc(const, 1)
            nc.gpsimd.memset(wvo[:, :, D:D + 1], 0.0).then_inc(const, 1)
            pool.wait_ge(const, 4)
            nc.gpsimd.memset(wvo[2 * R:VC, :, D:D + 1], 1.0).then_inc(const, 1)
            pool.wait_ge(const, 5)
            nc.gpsimd.memset(ones_row[:, :], 1.0).then_inc(const, 1)
            pool.wait_ge(const, 6)
            nc.gpsimd.memset(k_lo1[FEAT:FEAT + 2, :].bitcast(F32), 1.0).then_inc(const, 1)
            pool.wait_ge(const, 7)
            nc.gpsimd.affine_select(out=ident[:, :], in_=ident[:, :], compare_op=ALU.not_equal, fill=1.0,
                                    base=0, pattern=[[-1, P]], channel_multiplier=1).then_inc(const, 1)
            for c in range(NJ):
                pool.wait_ge(dve_k, c + 1)
                nc.gpsimd.tensor_copy(k_lo1[0:FEAT, chunk(c)], k_lo2[0:FEAT, chunk(c)]).then_inc(pool_k, 1)
            pool.wait_ge(dve_w, 6)
            nc.gpsimd.tensor_copy(wq_now[:, :], wq[:, 0, :]).then_inc(wq_ok, 1)
            pool.wait_ge(act_w, 5)
            pool.wait_ge(in_q, 16 * 9)
            nc.gpsimd.tensor_copy(qb_now[:, :], qbias[:, 0:1]).then_inc(wq_ok, 1)
            with pool.Fori(0, HEADS - 1) as t:
                pool.wait_ge(qlo_ok, t * NJ + NJ)
                nc.gpsimd.tensor_copy(wq_now[:, :], wq[:, bass.ds(t + 1, 1), :].rearrange("p a c -> p (a c)")).then_inc(wq_ok, 1)
                nc.gpsimd.tensor_copy(qb_now[:, :], qbias[:, bass.ds(t + 1, 1)]).then_inc(wq_ok, 1)
        @block.scalar
        def _(act):
            for t, d in ((uq4_sb[:, :, :], uq4), (ukb_sb[:, :, :], ukb), (buq_sb[:, :], buq)):
                act.dma_start(t, d).then_inc(in_q, 16)
            for r in range(4):
                act.dma_start(wqf[R * r:R * (r + 1), :, R:FEAT], wqr).then_inc(in_q, 16)
            for r in range(2):
                act.dma_start(qbias[FEAT * r + R:FEAT * (r + 1), :], bqr).then_inc(in_q, 16)

            act.wait_ge(in_k, 16 * (4 + NJ))
            for c in range(NJ):
                act.wait_ge(pe_k, c + 1)
                src = score[c // 2][:, (c % 2) * QB:(c % 2 + 1) * QB]
                nc.scalar.activation(kf[:, chunk(c)], src, ACT.Identity, bias=bk4_sb[:, 0:1]).then_inc(act_k, 1)
                nc.scalar.activation(k_hi2[:, chunk(c)], src, ACT.Identity, bias=bk4_sb[:, 0:1]).then_inc(act_k, 1)
            for c in range(NJ):
                act.wait_ge(pe_c, c + 1)
                src = mscore[:, (c % 2) * QB:(c % 2 + 1) * QB]
                nc.scalar.activation(cqf[:, chunk(c)], src, ACT.Identity, bias=bdq4_sb[:, 0:1]).then_inc(act_c, 1)
                nc.scalar.activation(cq_hl[:, chunk(c)], src, ACT.Identity, bias=bdq4_sb[:, 0:1]).then_inc(act_c, 1)
            act.wait_ge(pe_w, 1)
            wqp = misc[:, 0:HEADS * (R + 1)].rearrange("p (h c) -> p h c", h=HEADS)
            nc.scalar.copy(wqf[:, :, 0:R], wqp[:, :, 0:R]).then_inc(act_w, 1)
            nc.scalar.copy(uwf[:, :], wqp[:, :, R]).then_inc(act_w, 1)
            act.wait_ge(pe_w, 2)
            for r in range(2):
                nc.scalar.copy(qbias[FEAT * r:FEAT * r + R, :], ctx_ps[FEAT * r:FEAT * r + R, 0:HEADS]).then_inc(act_w, 1)
            nc.scalar.copy(uconst[:, :], ctx_ps[:, 2 * HEADS:3 * HEADS]).then_inc(act_w, 1)
            act.wait_ge(pe_w, 3)
            nc.scalar.copy(vf[:, :, :], score[0][:, 0:KT * R].rearrange("p (t r) -> p t r", t=KT)).then_inc(act_w, 1)
            nc.scalar.copy(vals[:, :, 0:R], score[0][:, 0:KT * R].rearrange("p (t r) -> p t r", t=KT)).then_inc(act_w, 1)
            act.wait_ge(pe_w, 4)
            nc.scalar.copy(wvo[:, :, 0:D],
                           score[1][0:VC, :].rearrange("p (h d) -> p h d", h=HEADS)).then_inc(act_w, 1)

            def queries(t, c):
                j = c % NJ
                act.wait_ge(proj_ok, nth(t, c) + 1)
                nc.scalar.activation(q_hl[j][:, :], misc[:, :], ACT.Identity, bias=qb_now[:, 0:1]).then_inc(qhi_ok, 1)
                nc.scalar.activation(q_hm[j][0:FEAT, :], misc[0:FEAT, :], ACT.Identity, bias=qb_now[0:FEAT, 0:1]).then_inc(qhi_ok, 1)

            def shift_row(t, c):
                act.wait_ge(row_ok, nth(t, c) + 1)
                nc.scalar.copy(q_hm[c % NJ][FEAT:FEAT + 2, :], misc[0:2, :]).then_inc(row_in, 1)

            def context(t, c):
                act.wait_ge(pv_ok, nstep(t, c, STEPS))
                nc.scalar.copy(ctx_sb[:, :], ctx_ps[0:VC, :]).then_inc(ctx_ok, 1)

            queries(0, 0)
            queries(0, 1)
            shift_row(0, 0)

            def body(t, c):
                for s in range(STEPS):
                    if s == 1 and not (isinstance(t, int) and NJ * t + c == 0):
                        context(t, c - 1)
                    act.wait_ge(score_ok, nstep(t, c, s) + 1)
                    if not (isinstance(t, int) and NJ * STEPS * t + c * STEPS + s < NPH):
                        act.wait_ge(pv_ok, nstep(t, c, s) - (NPH - 1))
                    nc.scalar.activation(p_hi[s % NPH][:, :], score[s % 2][:, :], ACT.Exp, scale=SCALE).then_inc(phi_ok, 1)
                    if not (isinstance(t, int) and NJ * STEPS * t + c * STEPS + s < 2):
                        act.wait_ge(plo_ok, nstep(t, c, s) - 1)
                    nc.scalar.activation(p_f[s % 2][:, :], score[s % 2][:, :], ACT.Exp, scale=SCALE).then_inc(pf_ok, 1)
                    if s == 2 and is_block(t, c + 2):
                        queries(t, c + 2)
                    if s == 6 and is_block(t, c + 1):
                        shift_row(t, c + 1)

            blocks(act, body)
            context(HEADS - 1, NJ - 1)

            act.wait_ge(ln, LN_VAR)
            nc.scalar.activation(std[:, :], mv[:, :, 1], ACT.Sqrt, bias=eps_col[:, 0:1]).then_inc(std_ok, 1)
            for j in range(NJ):
                act.wait_ge(x1T_ps, j + 1)
                nc.scalar.copy(x1T[:, chunk(j)], ctx_misc(j)).then_inc(x1T_ok, 1)
            with act.Fori(0, NJ) as i:
                for k in range(HT):
                    act.wait_ge(gate_ok, i * HT + (k + 1))
                    nc.scalar.activation(sil[:, k, :], gate_t(k), ACT.Silu).then_inc(sil_ok, 1)
            act.wait_ge(ln, LN_ALL + LN_VAR)
            nc.scalar.activation(std[:, :], mv[:, :, 1], ACT.Sqrt, bias=eps_col[:, 0:1]).then_inc(std_ok, 1)

        @block.vector
        def _(dve):
            dve.wait_ge(const, CONST_ALL)
            nc.vector.tensor_copy(ident_r[:, :], ident[:, :]).then_inc(ident_ok, 1)
            for c in range(NJ):
                dve.wait_ge(act_k, 2 * (c + 1))
                nc.vector.tensor_tensor(k_lo2[:, chunk(c)], kf[:, chunk(c)], k_hi2[:, chunk(c)], ALU.subtract).then_inc(dve_k, 1)
            for c in range(NJ):
                dve.wait_ge(act_c, 2 * (c + 1))
                for r in (1, 3):
                    part = slice(R * r, R * (r + 1))
                    nc.vector.tensor_tensor(cq_hl[part, chunk(c)], cqf[part, chunk(c)], cq_hl[part, chunk(c)],
                                            ALU.subtract).then_inc(dve_c, 1)
            dve.wait_ge(act_w, 2)
            dve.wait_ge(in_q, 16 * 9)
            for r in range(2):
                nc.vector.tensor_copy(wq[:, :, FEAT * r:FEAT * (r + 1)], wqf[:, :, :]).then_inc(dve_w, 1)
            nc.vector.tensor_copy(uw[:, :], uwf[:, :]).then_inc(dve_w, 1)
            dve.wait_ge(dve_w, 3)
            lo = slice(FEAT, 2 * FEAT)
            for r in range(2):
                cols = slice(FEAT * r, FEAT * (r + 1))
                nc.vector.tensor_tensor(wq[lo, :, cols], wqf[lo, :, :], wq[lo, :, cols], ALU.subtract).then_inc(dve_w, 1)
            nc.vector.tensor_tensor(uw[lo, :], uwf[lo, :], uw[lo, :], ALU.subtract).then_inc(dve_w, 1)
            dve.wait_ge(act_w, 7)
            nc.vector.tensor_tensor(vals[:, :, R:2 * R], vf[:, :, :], vals[:, :, 0:R], ALU.subtract).then_inc(dve_w, 1)
            dve.wait_ge(pe_w, 5)
            nc.vector.tensor_tensor(u[:, :].rearrange("p (h t) -> p h t", h=HEADS),
                                    ctx_ps[:, 0:KT * HEADS].rearrange("p (t h) -> p h t", h=HEADS),
                                    uconst[:, :].unsqueeze(2).to_broadcast([P, HEADS, KT]), ALU.add).then_inc(dve_w, 1)
            dve.wait_ge(in_x, 32)
            nc.vector.tensor_tensor(resid[:, :, :], resid[:, :, :],
                                    bo_sb[:, :].unsqueeze(1).to_broadcast([P, KT, D]), ALU.add).then_inc(dve_w, 1)

            def queries(t, c):
                j = c % NJ
                dve.wait_ge(qhi_ok, nth(t, c) * 2 + 2)
                nc.vector.scalar_tensor_tensor(out=q_hl[j][lo, :], in0=misc[lo, :], scalar=qb_now[lo, 0:1], in1=q_hl[j][lo, :],
                                               op0=ALU.add, op1=ALU.subtract).then_inc(qlo_ok, 1)

            def unit(c, k, n):
                dve.wait_ge(unit_ok, n + 1)
                nc.vector.reduce_max(mx_part[c % 2][:, k // 2, k % 2:k % 2 + 1], mscore[:, :], AX.X).then_inc(unit_max, 1)

            def shifts(t, c):
                j, b = c % NJ, nth(t, c)
                off = head_of(t, c) * KT + j * QT
                uj = u[:, off:off + QT] if isinstance(off, int) else u[:, bass.ds(off, QT)]
                dve.wait_ge(unit_max, b * UNITS + UNITS)
                nc.vector.reduce_max(mx[:, :], mx_part[c % 2][:, :, :], AX.X).then_inc(mchain, 1)
                dve.wait_ge(mchain, b * 4 + 1)
                nc.vector.tensor_tensor(mxu[:, :], mx[:, :], uj, ALU.add).then_inc(mchain, 1)
                dve.wait_ge(mchain, b * 4 + 2)
                nc.vector.tensor_tensor(shift[:, :], uj, mxu[:, :], ALU.subtract).then_inc(mchain, 1)
                dve.wait_ge(mchain, b * 4 + 3)
                nc.vector.tensor_copy(shift_hl[:, :, 0], shift[:, :]).then_inc(mchain, 1)
                dve.wait_ge(mchain, b * 4 + 4)
                nc.vector.tensor_tensor(shift_hl[:, :, 1], shift[:, :], shift_hl[:, :, 0], ALU.subtract).then_inc(shift_ok, 1)

            def add_context(t, c, half):
                j, n = c % NJ, nth(t, c) * 2 + half
                dve.wait_ge(outp_ok, n + 1)
                rd = rden[:, 2 * half:2 * half + 2]
                nc.vector.reciprocal(rd, outp[:, :, DEN]).then_inc(den_ok, 1)
                dve.wait_ge(den_ok, n + 1)
                for i in range(2):
                    tile = j * QT + 2 * half + i
                    nc.vector.scalar_tensor_tensor(out=resid[:, tile, :], in0=outp[:, i, 0:D],
                                                   scalar=rden[:, 2 * half + i:2 * half + i + 1], in1=resid[:, tile, :],
                                                   op0=ALU.mult, op1=ALU.add).then_inc(added, 1)

            dve.wait_ge(dve_w, 9)
            queries(0, 0)
            queries(0, 1)
            for n in range(AHEAD):
                if n == UNITS:
                    shifts(0, 0)
                unit(n // UNITS, n % UNITS, n)

            def body(t, c):
                for s in range(STEPS):
                    if s == 5 and is_block(t, c + 1):
                        shifts(t, c + 1)
                    k = s + AHEAD
                    if is_block(t, c + k // UNITS):
                        unit(c + k // UNITS, k % UNITS, nstep(t, c, k))
                    dve.wait_ge(pf_ok, nstep(t, c, s) + 1)
                    if not (isinstance(t, int) and NJ * STEPS * t + c * STEPS + s < NPH):
                        dve.wait_ge(pv_ok, nstep(t, c, s) - (NPH - 1))
                    nc.vector.tensor_tensor(p_lo[s % NPH][:, :], p_f[s % 2][:, :], p_hi[s % NPH][:, :],
                                            ALU.subtract).then_inc(plo_ok, 1)
                    if s == 2 and is_block(t, c + 2):
                        queries(t, c + 2)
                    if s in (3, 4) and not (isinstance(t, int) and NJ * t + c == 0):
                        add_context(t, c - 1, s - 3)

            blocks(dve, body)
            dve.wait_ge(in_f, 16 * 3)
            nc.vector.tensor_scalar(wffn[:, :], wint[:, :], WSCALE, None, ALU.mult).then_inc(ffw_ok, 1)
            for half in range(2):
                add_context(HEADS - 1, NJ - 1, half)
            dve.wait_ge(added, NB * QT)

            def layernorm(n):
                for q in range(KT):
                    nc.vector.bn_stats(stats[:, q, :], resid[:, q, :]).then_inc(ln, 1)
                dve.wait_ge(ln, n * LN_ALL + KT)
                for q in range(KT):
                    nc.vector.bn_aggr(mv[:, q, :], stats[:, q, :]).then_inc(ln, 1)
                dve.wait_ge(std_ok, n + 1)
                nc.vector.reciprocal(rstd[:, :], std[:, :]).then_inc(ln, 1)
                dve.wait_ge(ln, n * LN_ALL + LN_VAR + 1)
                for q in range(KT):
                    nc.vector.tensor_scalar(resid[:, q, :], resid[:, q, :], mv[:, q, 0:1], rstd[:, q:q + 1],
                                            ALU.subtract, ALU.mult).then_inc(ln, 1)

            layernorm(0)
            dve.wait_ge(ln, LN_ALL)
            nc.vector.memset(rden[:, :], 0.0).then_inc(y_ok, 1)
            with dve.Fori(0, NJ) as i:
                tokens = resid[:, bass.ds(i * QT, QT), :]
                for k in range(HT):
                    dve.wait_ge(sil_ok, i * HT + (k + 1))
                    nc.vector.tensor_tensor(hT[:, k, :], up_t(k), sil[:, k, :], ALU.mult).then_inc(h_ok, 1)
                dve.wait_ge(down_ok, i + 1)
                nc.vector.tensor_tensor(tokens, ctx_ps[:, :].rearrange("p (q d) -> p q d", q=QT),
                                        tokens, ALU.add).then_inc(y_ok, 1)
            dve.wait_ge(y_ok, NJ + 1)
            layernorm(1)

        @block.tensor
        def _(pe):
            pe.wait_ge(in_k, 16 * (4 + NJ))
            for c in range(NJ):
                nc.tensor.matmul(score[c // 2][:, (c % 2) * QB:(c % 2 + 1) * QB], wk4_sb[:, :], xT_sb[:, chunk(c)],
                                 start=True, stop=True).then_inc(pe_k, 1)
            for c in range(NJ):
                if c >= 2:
                    pe.wait_ge(act_c, 2 * (c - 1))
                nc.tensor.matmul(mscore[:, (c % 2) * QB:(c % 2 + 1) * QB], wdq4_sb[:, :], xT_sb[:, chunk(c)],
                                 start=True, stop=True).then_inc(pe_c, 1)
            pe.wait_ge(in_q, 16 * 9)
            for h in range(HEADS):
                last = nc.tensor.matmul(misc[:, h * (R + 1):(h + 1) * (R + 1)], uq4_sb[:, h, :], ukb_sb[:, h, :],
                                        start=True, stop=True)
            last.then_inc(pe_w, 1)
            for h in range(HEADS):
                for r in range(2):
                    nc.tensor.matmul(ctx_ps[FEAT * r:FEAT * r + R, h:h + 1], ukb_sb[:, h, 0:R], buq_sb[:, h:h + 1],
                                     start=True, stop=True)
            for h in range(HEADS):
                last = nc.tensor.matmul(ctx_ps[:, 2 * HEADS + h:2 * HEADS + h + 1],
                                        buq_sb[:, h:h + 1].to_broadcast([P, P]), ukb_sb[:, h, R:R + 1],
                                        start=True, stop=True)
            last.then_inc(pe_w, 1)
            pe.wait_ge(in_v, 16 * 4)
            pe.wait_ge(const, CONST_ALL)
            pe.wait_ge(act_k, 2 * NJ)
            for t in range(KT):
                o = score[0][:, t * R:(t + 1) * R]
                nc.tensor.matmul(o, xT_sb[:, t * P:(t + 1) * P], wdkv_sb[:, :], start=True, stop=False)
                last = nc.tensor.matmul(o, ones_row[:, :], bdkv_sb[:, :], start=False, stop=True)
            last.then_inc(pe_w, 1)
            for h in range(HEADS):
                last = nc.tensor.matmul(score[1][0:VC, h * D:(h + 1) * D], uvT2_sb[:, h, :], wo_sb[:, h, :],
                                        start=True, stop=True)
            last.then_inc(pe_w, 1)
            pe.wait_ge(dve_c, 2 * NJ)
            pe.wait_ge(dve_w, 6)
            pe.wait_ge(act_w, 5)
            for t in range(KT):
                last = nc.tensor.matmul(ctx_ps[:, t * HEADS:(t + 1) * HEADS], cq_hl[:, t * P:(t + 1) * P], uw[:, :],
                                        start=True, stop=True)
            last.then_inc(pe_w, 1)

            def project(t, c):
                if c % NJ == 0:
                    pe.wait_ge(wq_ok, head_of(t, c) * 2 + 2)
                nc.tensor.matmul(misc[:, :], wq_now[:, :], cq_hl[:, chunk(c % NJ)],
                                 start=True, stop=True).then_inc(proj_ok, 1)

            def unit(j, k):
                for cc in range(HALF // QB):
                    keys = slice((k % 2) * HALF + cc * QB, (k % 2) * HALF + (cc + 1) * QB)
                    o = mscore[:, cc * QB:(cc + 1) * QB]
                    qt = q_hl[j][:, (k // 2) * P:(k // 2 + 1) * P]
                    nc.tensor.matmul(o, qt, k_hi2[:, keys], start=True, stop=False)
                    last = nc.tensor.matmul(o, qt, k_lo2[:, keys], start=False, stop=True)
                last.then_inc(unit_ok, 1)

            def rows(t, c):
                pe.wait_ge(shift_ok, nth(t, c) + 1)
                for q in range(QT):
                    last = nc.tensor.matmul(misc[0:2, q * P:(q + 1) * P], shift_hl[:, q, :], ident_r[:, :],
                                            start=True, stop=True)
                last.then_inc(row_ok, 1)

            def scores(j, s):
                for a in range(2):
                    kt = slice((2 * s + a) * P, (2 * s + a + 1) * P)
                    o = score[s % 2][:, a * QB:(a + 1) * QB]
                    nc.tensor.matmul(o, k_hi2[:, kt], q_hl[j][:, :], start=True, stop=False)
                    last = nc.tensor.matmul(o, k_lo1[:, kt], q_hm[j][:, :], start=False, stop=True)
                last.then_inc(score_ok, 1)

            def contract(s):
                for a in range(2):
                    for n, part in enumerate((p_hi, p_lo)):
                        last = nc.tensor.matmul(ctx_ps[0:VC, :], vals[:, 2 * s + a, :],
                                                part[s % NPH][:, a * QB:(a + 1) * QB],
                                                start=(s == 0 and a == 0 and n == 0),
                                                stop=(s == STEPS - 1 and a == 1 and n == 1))
                last.then_inc(pv_ok, 1)

            def project_context(t, c, half):
                hd = head_of(t, c)
                rhs = wvo[:, hd, :] if isinstance(hd, int) else wvo[:, bass.ds(hd, 1), :].rearrange("p a d -> p (a d)")
                for i in range(2):
                    q = 2 * half + i
                    last = nc.tensor.matmul(outp[:, i, 0:D + 1], ctx_sb[:, q * P:(q + 1) * P], rhs, start=True, stop=True)
                last.then_inc(outp_ok, 1)

            pe.wait_ge(act_w, 8)
            pe.wait_ge(dve_k, NJ)
            project(0, 0)
            pe.wait_ge(qlo_ok, 1)
            project(0, 1)
            for n in range(AHEAD):
                if n == UNITS:
                    pe.wait_ge(qlo_ok, 2)
                if n:
                    pe.wait_ge(unit_max, n)
                unit(n // UNITS, n % UNITS)
            pe.wait_ge(ident_ok, 1)
            rows(0, 0)
            pe.wait_ge(row_in, 1)
            pe.wait_ge(pool_k, NJ)
            scores(0, 0)
            pe.wait_ge(dve_w, 8)

            def body(t, c):
                first = isinstance(t, int) and NJ * t + c == 0
                for s in range(STEPS):
                    k = s + AHEAD
                    if s == 2 and is_block(t, c + 2):
                        pe.wait_ge(row_in, nth(t, c) + 1)
                        project(t, c + 2)
                    if s == 6 and is_block(t, c + 1):
                        if first:
                            pe.wait_ge(qlo_ok, 3)
                        else:
                            pe.wait_ge(added, nth(t, c) * QT)
                        rows(t, c + 1)
                    if is_block(t, c + k // UNITS):
                        if k % UNITS == 0:
                            pe.wait_ge(qlo_ok, nth(t, c + k // UNITS) + 1)
                        pe.wait_ge(unit_max, nstep(t, c, k))
                        unit((c + k // UNITS) % NJ, k % UNITS)
                    nxt = c + (s + 1) // STEPS
                    if is_block(t, nxt):
                        if s == STEPS - 1:
                            pe.wait_ge(row_in, nth(t, c + 1) + 1)
                        if not (first and s == 0):
                            pe.wait_ge(pf_ok, nstep(t, c, s))
                        scores(nxt % NJ, (s + 1) % STEPS)
                    if not (first and s == 0):
                        pe.wait_ge(plo_ok, nstep(t, c, s))
                        if s == 1 and not first:
                            pe.wait_ge(ctx_ok, nth(t, c))
                        contract((s - 1) % STEPS)
                    if s in (3, 4) and not first:
                        if s == 3:
                            pe.wait_ge(ctx_ok, nth(t, c))
                            if is_block(t, c + 2):
                                pe.wait_ge(qlo_ok, nth(t, c + 2) + 1)
                            else:
                                pe.wait_ge(row_in, nth(t, c) + 1)
                        else:
                            pe.wait_ge(added, nth(t, c - 1) * QT + 2)
                        project_context(t, c - 1, s - 3)

            blocks(pe, body)
            pe.wait_ge(plo_ok, NB * STEPS)
            contract(STEPS - 1)
            pe.wait_ge(added, (NB - 1) * QT)
            pe.wait_ge(ctx_ok, NB)
            project_context(HEADS - 1, NJ - 1, 0)
            pe.wait_ge(added, (NB - 1) * QT + 2)
            project_context(HEADS - 1, NJ - 1, 1)

            pe.wait_ge(ffw_ok, 1)
            wd_t = wffn[:, 2 * H:2 * H + HT * D].rearrange("p (k d) -> p k d", k=HT)
            for j in range(NJ):
                pe.wait_ge(ln, LN_VAR + 1 + (j + 1) * QT)
                if j >= 2:
                    pe.wait_ge(x1T_ok, j - 1)
                for q in range(QT):
                    last = nc.tensor.transpose(ctx_misc(j)[:, q * P:(q + 1) * P], resid[:, j * QT + q, :], ident[:, :])
                last.then_inc(x1T_ps, 1)
            pe.wait_ge(x1T_ok, NJ)
            with pe.Fori(0, NJ) as i:
                xt = x1T[:, bass.ds(i * QB, QB)]
                pe.wait_ge(y_ok, i + 1)
                for k in range(HT):
                    nc.tensor.matmul(gate_t(k), wffn[:, k * P:(k + 1) * P], xt, start=True, stop=True)
                    nc.tensor.matmul(up_t(k), wffn[:, H + k * P:H + (k + 1) * P], xt,
                                     start=True, stop=True).then_inc(gate_ok, 1)
                pe.wait_ge(h_ok, i * HT + HT)
                for q in range(QT):
                    for k in range(HT):
                        last = nc.tensor.matmul(ctx_ps[:, q * D:(q + 1) * D], hT[:, k, q * P:(q + 1) * P], wd_t[:, k, :],
                                                start=(k == 0), stop=(k == HT - 1))
                last.then_inc(down_ok, 1)


def kernel(**inputs):
    import concourse.bacc as bacc
    from concourse.bass_utils import run_bass_kernel_spmd

    a = {n.replace("L0_attn_", "").replace("L0_ffn_", ""): np.asarray(v) for n, v in inputs.items()}
    b, s, d = a["h_t"].shape
    r = a["W_DKV"].shape[1]
    heads = a["b_QR"].shape[0] // r
    dk = a["W_UK"].shape[1] // heads
    ht = a["w_down"].shape[1] // d

    def cat(*parts):
        return np.concatenate(parts, axis=-1)

    def by_head(w):
        return w.reshape(r, heads, dk).transpose(2, 1, 0)

    def col(v):
        return v.reshape(-1, 1)

    x = a["h_t"].reshape(s, d)
    laid = {
        "x": x,
        "xT": x.T,
        "wdq4": cat(*[a["W_DQ"]] * 4),
        "wk4": cat(a["W_DKV"], a["W_KR"], a["W_DKV"], a["W_KR"]),
        "wdkv": a["W_DKV"],
        "bdq4": col(cat(*[a["b_DQ"]] * 4)),
        "bk4": col(cat(a["b_DKV"], a["b_KR"], a["b_DKV"], a["b_KR"])),
        "bdkv": a["b_DKV"].reshape(1, r),
        "uq4": cat(*[by_head(a["W_UQ"])] * 4),
        "ukb": cat(by_head(a["W_UK"]), a["b_UK"].reshape(heads, dk).T[:, :, None]),
        "buq": a["b_UQ"].reshape(heads, dk).T,
        "wqr": a["W_QR"].reshape(r, heads, r),
        "bqr": a["b_QR"].reshape(heads, r).T,
        "uvT2": cat(by_head(a["W_UV"]), by_head(a["W_UV"]), a["b_UV"].reshape(heads, dk).T[:, :, None]),
        "wo": a["W_O"].reshape(heads, dk, d).transpose(1, 0, 2),
        "bo": a["b_O"],
        "wg": a["w_gate"].T,
        "wu": a["w_up"].T,
        "wd": a["w_down"].T.reshape(ht, d, d).transpose(1, 0, 2),
    }
    nc = bacc.Bacc("TRN2", target_bir_lowering=False, num_devices=1)
    arrays, args = {}, []
    for n, v in laid.items():
        arrays[f"in_{n}"] = np.ascontiguousarray(v)
        args.append(nc.dram_tensor(f"in_{n}", v.shape, mybir.dt.from_np(v.dtype), kind="ExternalInput").ap())
    args.append(nc.dram_tensor("out_0", (s, d), F32, kind="ExternalOutput").ap())
    attention_ffn(nc, *args)
    res = run_bass_kernel_spmd(nc, [arrays], core_ids=[0])
    return res.results[0]["out_0"].reshape(b, s, d)
```

```python
import numpy as np
import concourse.bass as bass
from concourse import mybir
from contextlib import ExitStack

F32 = mybir.dt.float32
F32R = mybir.dt.float32r
I32 = mybir.dt.int32
BF16 = mybir.dt.bfloat16
ALU = mybir.AluOpType
ACT = mybir.ActivationFunctionType
AX = mybir.AxisListType


def attention_ffn(nc, x, xT, wlat, blat, uq4, ukb, buq, wqr4, qb0, uv2, wo, bo, wg, wu, wd, out):
    P = 128
    S = x.shape[0]
    D = x.shape[1]
    HEADS = uq4.shape[1]
    R = uq4.shape[2] // 4
    FEAT = 2 * R
    QB = 512
    NJ = S // QB
    NB = HEADS * NJ
    QT = QB // P
    KT = S // P
    STEPS = KT // 2
    HALF = S // 2
    UNITS = 2 * QT
    AHEAD = UNITS + 3
    LO_AT = {3: 1, 5: 3, 7: 5, 0: 7}
    POOL_STEPS = (2, 4, 5)
    HI, SUM, LO, SUM2 = 0, R, 2 * R, 3 * R
    CR = SUM2 + 1
    DEN = D
    OC = D + 2
    H = wg.shape[1]
    HT = H // P
    SCALE = 1.0 / float(np.sqrt(P + R))
    WSCALE = float(np.float32(1.0 / 127.0))
    EPS = 1e-5
    assert UNITS == STEPS and D == P and x.shape[1] == P

    ctx = ExitStack()
    with ctx:
        def sb(name, shape, dt=F32):
            return ctx.enter_context(nc.sbuf_tensor(name, shape, dt))

        def ps(name, shape):
            return ctx.enter_context(nc.psum_tensor(name, shape, F32))

        def sem(name):
            return ctx.enter_context(nc.semaphore(name))

        xT_sb = sb("xT_sb", [P, S])
        resid = sb("resid", [P, KT, D])
        bo_sb = sb("bo_sb", [P, D])
        wlat_sb = sb("wlat_sb", [P, 2, 4 * R])
        blat_sb = sb("blat_sb", [P, 2])
        uq4_sb = sb("uq4_sb", [P, HEADS, 4 * R])
        ukb_sb = sb("ukb_sb", [P, HEADS, R + 1])
        buq_sb = sb("buq_sb", [P, HEADS])
        uv2_sb = sb("uv2_sb", [P, HEADS, CR])
        wo_sb = sb("wo_sb", [P, HEADS, D])
        wint = sb("wint", [P, 2 * H + HT * D], I32)
        wffn = sb("wffn", [P, 2 * H + HT * D])
        wf_hi = sb("wf_hi", [P, 2 * H + HT * D], F32R)
        wf_lo = sb("wf_lo", [P, 2 * H + HT * D], F32R)

        ident = sb("ident", [P, P])
        ident_r = sb("ident_r", [P, P], F32R)
        ones = sb("ones", [P, P])
        mhalf = sb("mhalf", [P, KT])

        k_hi2 = sb("k_hi2", [P, S], F32R)
        k_lo2 = sb("k_lo2", [P, S], F32R)
        k_lo1 = sb("k_lo1", [FEAT + 2, S], F32R)
        cq_hl = sb("cq_hl", [P, S], F32R)
        vals = sb("vals", [P, KT, P], F32R)
        vals_b = sb("vals_b", [P, KT, FEAT], BF16)
        wqf = sb("wqf", [P, HEADS, FEAT])
        wq = sb("wq", [P, HEADS, FEAT], F32R)
        wq_now = sb("wq_now", [P, 2 * FEAT], F32R)
        qb_now = sb("qb_now", [P, 1])
        qbias = sb("qbias", [P, HEADS])
        uwf = sb("uwf", [P, HEADS])
        uw = sb("uw", [P, HEADS], F32R)
        uconst = sb("uconst", [P, HEADS])
        u = sb("u", [P, HEADS * KT])
        ub = sb("ub", [P, HEADS])
        wvof = sb("wvof", [CR, HEADS, OC])
        wvo_hi = sb("wvo_hi", [CR, HEADS, OC], F32R)
        wvo_lo = sb("wvo_lo", [CR, HEADS, OC], F32R)

        q_hl = [sb(f"q_hl{j}", [P, QB], F32R) for j in range(NJ)]
        q_hm = [sb(f"q_hm{j}", [FEAT + 2, QB], F32R) for j in range(NJ)]
        mx_part = [sb(f"mx_part{j}", [P, QT, 4]) for j in range(2)]
        mx = sb("mx", [P, QT])
        mxu = sb("mxu", [P, QT])
        shift = sb("shift", [P, QT])
        shift_hl = sb("shift_hl", [P, QT, 2], F32R)
        NPH = 4
        p_hi = [sb(f"p_hi{n}", [P, 2 * QB], F32R) for n in range(NPH)]
        p_lo = [sb(f"p_lo{n}", [P, 2 * QB], BF16) for n in range(NPH)]
        NPF = 4
        p_f = [sb(f"p_f{n}", [P, 2 * QB]) for n in range(NPF)]
        ctx_hi = sb("ctx_hi", [CR, QB], F32R)
        ctx_lo = sb("ctx_lo", [CR, QB], F32R)
        rden = sb("rden", [P, QT])

        score = [ps(f"score{n}", [P, 2 * QB]) for n in range(2)]
        mscore = ps("mscore", [P, HALF])
        ctx_ps = ps("ctx_ps", [P, QB])
        misc = ps("misc", [P, QB])
        outp = misc[:, :].rearrange("p (t c) -> p t c", t=2)

        stats = sb("stats", [P, KT, 6])
        mv = sb("mv", [P, KT, 2])
        veps = sb("veps", [P, KT])
        rstd = sb("rstd", [P, KT])
        x1_hi = cq_hl
        x1_lo = sb("x1_lo", [P, S], F32R)
        h_f = sb("h_f", [P, HT, QB])
        hidden_hi = (k_hi2, k_lo2)
        h_hi = [t[:, 0:HT * QB].rearrange("p (k q) -> p k q", k=HT) for t in hidden_hi]
        h_lo_sb = sb("h_lo_sb", [P, 2, HT, QB], F32R)
        h_lo = [h_lo_sb[:, n] for n in range(2)]
        sil = sb("sil", [P, HT, QB])

        in_k = sem("in_k")
        in_t = [sem(f"in_t{c}") for c in range(NJ)]
        in_q = sem("in_q")
        in_v = sem("in_v")
        in_x = sem("in_x")
        in_f = sem("in_f")
        const = sem("const")
        ident_ok = sem("ident_ok")
        pool_r = sem("pool_r")
        pe_k = sem("pe_k")
        act_k = sem("act_k")
        dve_k = sem("dve_k")
        lo1_ok = sem("lo1_ok")
        pe_c = sem("pe_c")
        act_c = sem("act_c")
        dve_c = sem("dve_c")
        pe_w = sem("pe_w")
        act_w = sem("act_w")
        dve_w = sem("dve_w")
        u_ok = sem("u_ok")
        wvo_ok = sem("wvo_ok")
        wq_ok = sem("wq_ok")
        proj_ok = sem("proj_ok")
        qhi_ok = sem("qhi_ok")
        qlo_ok = sem("qlo_ok")
        unit_ok = sem("unit_ok")
        unit_max = sem("unit_max")
        mchain = sem("mchain")
        shift_ok = sem("shift_ok")
        row_ok = sem("row_ok")
        row_in = sem("row_in")
        score_ok = sem("score_ok")
        phi_ok = sem("phi_ok")
        pf_ok = sem("pf_ok")
        plo_dve = sem("plo_dve")
        plo_pool = sem("plo_pool")
        pvhi_ok = sem("pvhi_ok")
        pvlo_ok = sem("pvlo_ok")
        ctx_ok = sem("ctx_ok")
        ctxlo_ok = sem("ctxlo_ok")
        outp_ok = sem("outp_ok")
        den_ok = sem("den_ok")
        added = sem("added")
        ffw_ok = sem("ffw_ok")
        ln = sem("ln")
        pool_ln = sem("pool_ln")
        x1T_ps = sem("x1T_ps")
        x1T_ok = sem("x1T_ok")
        x1lo_ok = sem("x1lo_ok")
        gate_ok = sem("gate_ok")
        up_ok = sem("up_ok")
        sil_ok = sem("sil_ok")
        h_ok = sem("h_ok")
        hhi_ok = sem("hhi_ok")
        hlo_ok = sem("hlo_ok")
        down_ok = sem("down_ok")
        y_ok = sem("y_ok")
        out_ok = sem("out_ok")

        block = ctx.enter_context(nc.Block())
        resid_v = x.rearrange("(t p) d -> p t d", p=P)
        out_v = out.rearrange("(t p) d -> p t d", p=P)

        def chunk(c):
            return slice(c * QB, (c + 1) * QB)

        def blocks(eng, body):
            body(0, 0)
            with eng.Fori(0, HEADS - 1) as t:
                for c in range(1, NJ + 1):
                    body(t, c)
            for c in range(NB - NJ + 1, NB):
                body(HEADS - 1, c - NB + NJ)

        def is_block(t, c):
            return not isinstance(t, int) or 0 <= NJ * t + c < NB

        def is_last(t):
            return isinstance(t, int) and t == HEADS - 1

        def nth(t, c):
            return t * NJ + c

        def nstep(t, c, s):
            return t * (NJ * STEPS) + (c * STEPS + s)

        def nhalf(t, c, k, i):
            return t * (NJ * UNITS * 2) + ((c * UNITS + k) * 2 + i)

        def wait_lo(eng, t, c, s):
            c, s = c + s // STEPS, s % STEPS
            pool = len([k for k in POOL_STEPS if k <= s])
            n = len(POOL_STEPS)
            if s in POOL_STEPS:
                eng.wait_ge(plo_pool, t * (NJ * n) + (c * n + pool))
            else:
                n = STEPS - n
                eng.wait_ge(plo_dve, t * (NJ * n) + (c * n + s + 1 - pool))

        def wait_used(eng, t, c, s):
            eng.wait_ge(pvlo_ok, t * (NJ * STEPS // 2) + (c * STEPS + s - NPH) // 2 + 1)

        def first_use(t, c):
            return c == 1 and not isinstance(t, int)

        def step_index(t, c, s):
            return NJ * STEPS * t + c * STEPS + s if isinstance(t, int) else STEPS * NJ

        def head_of(t, c):
            return t + c // NJ

        def gate_t(k):
            return (score[0][:, 0:QB], score[0][:, QB:2 * QB], score[1][:, 0:QB])[k]

        def up_t(k):
            return (score[1][:, QB:2 * QB], mscore[:, 0:QB], mscore[:, QB:2 * QB])[k]

        def down_t(j):
            return ctx_ps[:, :]

        EARLY = [score[0], score[1], mscore]
        early = [EARLY[n % len(EARLY)] for n in range(AHEAD)]

        HH = HEADS // 2
        IN_Q = 16 * 5
        DVE_W_ALL = 6
        ACT_W_ALL = 13
        CONST_ALL = 12

        LN_VAR = 2 * QT
        LN_ALL = LN_VAR + QT

        @block.sync
        def _(sp):
            for t, d in ((wlat_sb[:, :, :], wlat), (blat_sb[:, :], blat)):
                sp.dma_start(t, d).then_inc(in_k, 16)
            for c in range(NJ):
                sp.dma_start(xT_sb[:, chunk(c)], xT[:, chunk(c)]).then_inc(in_t[c], 16)
            for t, d in ((uv2_sb[:, :, :], uv2), (wo_sb[:, :, :], wo)):
                sp.dma_start(t, d).then_inc(in_v, 16)
            sp.dma_start(bo_sb[:, :], bo.partition_broadcast(P)).then_inc(in_x, 16)
            sp.dma_start(resid[:, :, :], resid_v).then_inc(in_x, 16)
            for t, d in ((wint[:, 0:H], wg), (wint[:, H:2 * H], wu),
                         (wint[:, 2 * H:2 * H + HT * D].rearrange("p (k d) -> p k d", k=HT), wd)):
                sp.dma_start(t, d).then_inc(in_f, 16)
            for j in range(NJ):
                sp.wait_ge(ln, (NJ + j + 1) * LN_ALL)
                sp.dma_start(out_v[:, j * QT:(j + 1) * QT, :], resid[:, j * QT:(j + 1) * QT, :]).then_inc(out_ok, 16)
            sp.wait_ge(out_ok, 16 * NJ)

        @block.gpsimd
        def _(pool):
            nc.gpsimd.memset(ident[:, :], 0.0).then_inc(const, 1)
            nc.gpsimd.memset(ones[:, :], 1.0).then_inc(const, 1)
            nc.gpsimd.memset(mhalf[:, :], -0.5).then_inc(const, 1)
            nc.gpsimd.memset(vals[:, :, SUM:LO].bitcast(F32), 0.0).then_inc(const, 1)
            nc.gpsimd.memset(vals[:, :, SUM2:P].bitcast(F32), 0.0).then_inc(const, 1)
            nc.gpsimd.memset(vals_b[:, :, SUM:FEAT], 0.0).then_inc(const, 1)
            nc.gpsimd.memset(wvof[:, :, D:OC], 0.0).then_inc(const, 1)
            pool.wait_ge(const, 7)
            nc.gpsimd.memset(vals[:, :, SUM:SUM + 1].bitcast(F32), 1.0).then_inc(const, 1)
            nc.gpsimd.memset(vals_b[:, :, SUM:SUM + 1], 1.0).then_inc(const, 1)
            pool.wait_ge(const, 9)
            nc.gpsimd.memset(wvof[SUM:SUM + 1, :, DEN:DEN + 1], 1.0).then_inc(const, 1)
            pool.wait_ge(const, 10)
            nc.gpsimd.memset(wvof[SUM2:CR, :, DEN:DEN + 1], 1.0).then_inc(const, 1)
            pool.wait_ge(const, 11)
            nc.gpsimd.affine_select(out=ident[:, :], in_=ident[:, :], compare_op=ALU.not_equal, fill=1.0,
                                    base=0, pattern=[[-1, P]], channel_multiplier=1).then_inc(const, 1)
            def twice(t):
                return t[:, :].rearrange("p (n c) -> p n c", n=2)

            pool.wait_ge(dve_w, DVE_W_ALL)
            nc.gpsimd.tensor_copy(twice(wq_now), wq[:, 0:1, :].to_broadcast([P, 2, FEAT])).then_inc(wq_ok, 1)
            pool.wait_ge(act_w, 5)
            pool.wait_ge(in_q, IN_Q)
            nc.gpsimd.tensor_copy(qb_now[:, :], qbias[:, 0:1]).then_inc(wq_ok, 1)
            pool.wait_ge(act_w, ACT_W_ALL)
            nc.gpsimd.tensor_copy(wvo_hi[:, :, :], wvof[:, :, :]).then_inc(wvo_ok, 1)
            pool.wait_ge(wvo_ok, 1)
            nc.gpsimd.tensor_tensor(wvo_lo[:, :, :], wvof[:, :, :], wvo_hi[:, :, :], ALU.subtract).then_inc(wvo_ok, 1)
            pool.wait_ge(in_x, 32)
            nc.gpsimd.tensor_tensor(resid[:, :, :], resid[:, :, :],
                                    bo_sb[:, :].unsqueeze(1).to_broadcast([P, KT, D]), ALU.add).then_inc(pool_r, 1)
            pool.wait_ge(in_f, 16 * 3)
            nc.gpsimd.tensor_scalar(wffn[:, :], wint[:, :], WSCALE, None, ALU.mult).then_inc(ffw_ok, 1)
            pool.wait_ge(ffw_ok, 1)
            nc.gpsimd.tensor_copy(wf_hi[:, :], wffn[:, :]).then_inc(ffw_ok, 1)
            pool.wait_ge(ffw_ok, 2)
            nc.gpsimd.tensor_tensor(wf_lo[:, :], wffn[:, :], wf_hi[:, :], ALU.subtract).then_inc(ffw_ok, 1)

            def rsqrt(n):
                cols = slice((n % NJ) * QT, (n % NJ + 1) * QT)
                pool.wait_ge(ln, n * LN_ALL + LN_VAR)
                nc.gpsimd.tensor_scalar(veps[:, cols], mv[:, cols, 1], EPS, None, ALU.add).then_inc(pool_ln, 1)
                pool.wait_ge(pool_ln, 2 * n + 1)
                nc.gpsimd.tensor_tensor(rstd[:, cols], veps[:, cols], mhalf[:, cols], ALU.pow).then_inc(pool_ln, 1)

            def body(t, c):
                for s in range(STEPS):
                    if s in POOL_STEPS:
                        pool.wait_ge(pf_ok, nstep(t, c, s) + 1)
                        if step_index(t, c, s) >= NPH:
                            wait_used(pool, t, c, s)
                        nc.gpsimd.tensor_tensor(p_lo[s % NPH][:, :], p_f[s % NPF][:, :], p_hi[s % NPH][:, :],
                                                ALU.subtract).then_inc(plo_pool, 1)
                    if s == STEPS - 2 and c == 1 and not isinstance(t, int):
                        pool.wait_ge(qlo_ok, t * NJ + NJ)
                        nc.gpsimd.tensor_copy(twice(wq_now),
                                              wq[:, bass.ds(t + 1, 1), :].to_broadcast([P, 2, FEAT])).then_inc(wq_ok, 1)
                        nc.gpsimd.tensor_copy(qb_now[:, :], qbias[:, bass.ds(t + 1, 1)]).then_inc(wq_ok, 1)
                    if s == STEPS - 2 and is_last(t):
                        rsqrt(c - 1)

            blocks(pool, body)
            rsqrt(NJ - 1)
            for j in range(NJ):
                for k in range(HT):
                    pool.wait_ge(hhi_ok, j * HT + k + 1)
                    if j >= 2:
                        pool.wait_ge(down_ok, j - 1)
                    nc.gpsimd.tensor_tensor(h_lo[j % 2][:, k, :], h_f[:, k, :], h_hi[j % 2][:, k, :],
                                            ALU.subtract).then_inc(hlo_ok, 1)
                if j >= 1:
                    rsqrt(NJ + j - 1)
            rsqrt(2 * NJ - 1)

        @block.scalar
        def _(act):
            for t, d in ((uq4_sb[:, :, :], uq4), (ukb_sb[:, :, :], ukb), (buq_sb[:, :], buq),
                         (wqf[:, :, R:FEAT], wqr4), (qbias[:, :], qb0)):
                act.dma_start(t, d).then_inc(in_q, 16)
            act.wait_ge(pe_w, 1)
            wqp = misc[:, 0:HEADS * (R + 1)].rearrange("p (h c) -> p h c", h=HEADS)
            nc.scalar.copy(wqf[:, :, 0:R], wqp[:, :, 0:R]).then_inc(act_w, 1)
            nc.scalar.copy(uwf[:, :], wqp[:, :, R]).then_inc(act_w, 1)
            act.wait_ge(pe_w, 2)
            act.wait_ge(in_q, IN_Q)
            for r in range(2):
                nc.scalar.copy(qbias[FEAT * r:FEAT * r + R, :], ctx_ps[0:R, 0:HEADS]).then_inc(act_w, 1)
            nc.scalar.copy(uconst[:, :], ctx_ps[:, HEADS:2 * HEADS]).then_inc(act_w, 1)
            act.wait_ge(in_k, 16 * 2)

            def keys(c):
                act.wait_ge(pe_k, c + 1)
                src = score[c // 2][:, (c % 2) * QB:(c % 2 + 1) * QB]
                nc.scalar.activation(k_hi2[:, chunk(c)], src, ACT.Identity, bias=blat_sb[:, 1:2]).then_inc(act_k, 1)

            def latent_queries(c):
                act.wait_ge(pe_c, c + 1)
                src = mscore[:, (c % 2) * QB:(c % 2 + 1) * QB]
                nc.scalar.activation(cq_hl[:, chunk(c)], src, ACT.Identity, bias=blat_sb[:, 0:1]).then_inc(act_c, 1)

            for c in range(NJ):
                if c < 2:
                    latent_queries(c)
                keys(c)

            def queries(t, c):
                j = c % NJ
                act.wait_ge(proj_ok, nth(t, c) + 1)
                nc.scalar.activation(q_hl[j][:, :], misc[:, :], ACT.Identity, bias=qb_now[:, 0:1]).then_inc(qhi_ok, 1)
                nc.scalar.activation(q_hm[j][0:FEAT, :], misc[0:FEAT, :], ACT.Identity, bias=qb_now[0:FEAT, 0:1]).then_inc(qhi_ok, 1)

            def shift_row(t, c):
                act.wait_ge(row_ok, nth(t, c) + 1)
                nc.scalar.copy(q_hm[c % NJ][FEAT:FEAT + 2, :], misc[0:2, :]).then_inc(row_in, 1)

            def context(t, c):
                act.wait_ge(pvlo_ok, t * (NJ * STEPS // 2) + (c + 1) * (STEPS // 2))
                nc.scalar.copy(ctx_hi[:, :], ctx_ps[0:CR, :]).then_inc(ctx_ok, 1)

            queries(0, 0)
            for c in range(2, NJ):
                latent_queries(c)
            for n in range(2):
                if n == 1:
                    queries(0, 1)
                act.wait_ge(pe_w, 3 + n)
                vp = ctx_ps[:, :].rearrange("p (t c) -> p t c", t=KT // 2)
                kt = slice(n * KT // 2, (n + 1) * KT // 2)
                nc.scalar.copy(vals[:, kt, HI:HI + R], vp[:, :, 0:R]).then_inc(act_w, 1)
                nc.scalar.copy(vals[:, kt, LO:LO + R], vp[:, :, R:2 * R]).then_inc(act_w, 1)
                nc.scalar.copy(vals_b[:, kt, 0:R], vp[:, :, 0:R]).then_inc(act_w, 1)
            for n in range(2):
                act.wait_ge(pe_w, 5 + n)
                nc.scalar.copy(wvof[:, n * HH:(n + 1) * HH, 0:D],
                               ctx_ps[0:CR, :].rearrange("p (h d) -> p h d", h=HH)).then_inc(act_w, 1)
            act.wait_ge(dve_k, NJ)
            for c in range(NJ):
                nc.scalar.copy(k_lo1[0:FEAT, chunk(c)], k_lo2[0:FEAT, chunk(c)]).then_inc(lo1_ok, 1)
            shift_row(0, 0)

            def body(t, c):
                for s in range(STEPS):
                    if s == 1 and not (isinstance(t, int) and NJ * t + c == 0):
                        context(t, c - 1)
                    act.wait_ge(score_ok, nstep(t, c, s) + 1)
                    if step_index(t, c, s) >= NPH:
                        act.wait_ge(pvhi_ok, nstep(t, c, s) - (NPH - 1))
                        wait_lo(act, t, c, s - NPH)
                    nc.scalar.activation(p_hi[s % NPH][:, :], score[s % 2][:, :], ACT.Exp, scale=SCALE).then_inc(phi_ok, 1)
                    nc.scalar.activation(p_f[s % NPF][:, :], score[s % 2][:, :], ACT.Exp, scale=SCALE).then_inc(pf_ok, 1)
                    if s == 2 and is_block(t, c + 2):
                        queries(t, c + 2)
                    if s == 6 and is_block(t, c + 1):
                        shift_row(t, c + 1)
                    if s == STEPS - 1 and is_last(t):
                        transposed(c - 1)

            def transposed(j):
                act.wait_ge(x1T_ps, j + 1)
                nc.scalar.copy(x1_hi[:, chunk(j)], misc[:, :]).then_inc(x1T_ok, 1)

            blocks(act, body)
            context(HEADS - 1, NJ - 1)

            for j in range(NJ):
                if j == NJ - 1:
                    transposed(j)
                for k in range(HT):
                    act.wait_ge(gate_ok, j * HT + k + 1)
                    nc.scalar.activation(sil[:, k, :], gate_t(k), ACT.Silu).then_inc(sil_ok, 1)
                for k in range(HT):
                    act.wait_ge(h_ok, j * HT + k + 1)
                    if j >= 2:
                        act.wait_ge(down_ok, j - 1)
                    nc.scalar.copy(h_hi[j % 2][:, k, :], h_f[:, k, :]).then_inc(hhi_ok, 1)

        @block.vector
        def _(dve):
            dve.wait_ge(const, CONST_ALL)
            nc.vector.tensor_copy(ident_r[:, :], ident[:, :]).then_inc(ident_ok, 1)
            nc.vector.memset(k_lo1[FEAT:FEAT + 2, :].bitcast(F32), 1.0).then_inc(ident_ok, 1)
            dve.wait_ge(in_q, IN_Q)
            nc.vector.tensor_tensor(ub[:, :], buq_sb[:, :], ukb_sb[:, :, R], ALU.mult).then_inc(u_ok, 1)
            dve.wait_ge(act_w, 2)
            dve.wait_ge(in_q, IN_Q)
            nc.vector.tensor_copy(wq[:, :, :], wqf[:, :, :]).then_inc(dve_w, 1)
            nc.vector.tensor_copy(uw[:, :], uwf[:, :]).then_inc(dve_w, 1)
            dve.wait_ge(dve_w, 2)
            for r in (1, 3):
                part = slice(R * r, R * (r + 1))
                nc.vector.tensor_tensor(wq[part, :, :], wqf[part, :, :], wq[part, :, :], ALU.subtract).then_inc(dve_w, 1)
                nc.vector.tensor_tensor(uw[part, :], uwf[part, :], uw[part, :], ALU.subtract).then_inc(dve_w, 1)
            lo = slice(FEAT, 2 * FEAT)

            def keys(c):
                dve.wait_ge(act_k, c + 1)
                src = score[c // 2][:, (c % 2) * QB:(c % 2 + 1) * QB]
                nc.vector.scalar_tensor_tensor(out=k_lo2[:, chunk(c)], in0=src, scalar=blat_sb[:, 1:2],
                                               in1=k_hi2[:, chunk(c)], op0=ALU.add, op1=ALU.subtract).then_inc(dve_k, 1)

            def latent_queries(c):
                dve.wait_ge(act_c, c + 1)
                src = mscore[:, (c % 2) * QB:(c % 2 + 1) * QB]
                nc.vector.scalar_tensor_tensor(out=cq_hl[lo, chunk(c)], in0=src[lo, :], scalar=blat_sb[lo, 0:1],
                                               in1=cq_hl[lo, chunk(c)], op0=ALU.add, op1=ALU.subtract).then_inc(dve_c, 1)

            dve.wait_ge(in_k, 16 * 2)
            for c in range(NJ):
                if c < 2:
                    latent_queries(c)
                keys(c)

            def queries(t, c):
                j = c % NJ
                dve.wait_ge(qhi_ok, nth(t, c) * 2 + 2)
                nc.vector.scalar_tensor_tensor(out=q_hl[j][lo, :], in0=misc[lo, :], scalar=qb_now[lo, 0:1], in1=q_hl[j][lo, :],
                                               op0=ALU.add, op1=ALU.subtract).then_inc(qlo_ok, 1)

            def unit(t, c, k, src=mscore):
                for i in range(2):
                    col = (k % 2) * 2 + i
                    dve.wait_ge(unit_ok, nhalf(t, c, k, i) + 1)
                    nc.vector.reduce_max(mx_part[(c + k // UNITS) % 2][:, k % UNITS // 2, col:col + 1],
                                         src[:, i * QB:(i + 1) * QB], AX.X).then_inc(unit_max, 1)

            def shifts(t, c):
                j, b = c % NJ, nth(t, c)
                off = head_of(t, c) * KT + j * QT
                uj = u[:, off:off + QT] if isinstance(off, int) else u[:, bass.ds(off, QT)]
                dve.wait_ge(unit_max, nhalf(t, c, UNITS, 0))
                nc.vector.reduce_max(mx[:, :], mx_part[c % 2][:, :, :], AX.X).then_inc(mchain, 1)
                dve.wait_ge(mchain, b * 4 + 1)
                nc.vector.tensor_tensor(mxu[:, :], mx[:, :], uj, ALU.add).then_inc(mchain, 1)
                dve.wait_ge(mchain, b * 4 + 2)
                nc.vector.tensor_tensor(shift[:, :], uj, mxu[:, :], ALU.subtract).then_inc(mchain, 1)
                dve.wait_ge(mchain, b * 4 + 3)
                nc.vector.tensor_copy(shift_hl[:, :, 0], shift[:, :]).then_inc(mchain, 1)
                dve.wait_ge(mchain, b * 4 + 4)
                nc.vector.tensor_tensor(shift_hl[:, :, 1], shift[:, :], shift_hl[:, :, 0], ALU.subtract).then_inc(shift_ok, 1)

            def add_context(t, c, half):
                j, n = c % NJ, nth(t, c) * 2 + half
                dve.wait_ge(outp_ok, n + 1)
                rd = rden[:, 2 * half:2 * half + 2]
                nc.vector.reciprocal(rd, outp[:, :, DEN]).then_inc(den_ok, 1)
                dve.wait_ge(den_ok, n + 1)
                for i in range(2):
                    tile = j * QT + 2 * half + i
                    nc.vector.scalar_tensor_tensor(out=resid[:, tile, :], in0=outp[:, i, 0:D],
                                                   scalar=rden[:, 2 * half + i:2 * half + i + 1], in1=resid[:, tile, :],
                                                   op0=ALU.mult, op1=ALU.add).then_inc(added, 1)

            queries(0, 0)
            for n in range(AHEAD):
                unit(0, 0, n, early[n])
                if n in (0, 1):
                    latent_queries(n + 2)
                if n == 4:
                    queries(0, 1)
                if n == UNITS - 1:
                    dve.wait_ge(pe_w, 7)
                    nc.vector.tensor_tensor(u[:, :].rearrange("p (h t) -> p h t", h=HEADS),
                                            ctx_ps[:, 0:KT * HEADS].rearrange("p (t h) -> p h t", h=HEADS),
                                            uconst[:, :].unsqueeze(2).to_broadcast([P, HEADS, KT]), ALU.add).then_inc(u_ok, 1)
                    dve.wait_ge(u_ok, 2)
                if n == UNITS - 1:
                    shifts(0, 0)
            dve.wait_ge(pool_r, 1)

            def body(t, c):
                for s in range(STEPS):
                    if s == 5 and is_block(t, c + 1):
                        shifts(t, c + 1)
                    k = s + AHEAD
                    if is_block(t, c + k // UNITS):
                        unit(t, c, k)
                    if s not in POOL_STEPS:
                        dve.wait_ge(pf_ok, nstep(t, c, s) + 1)
                        if step_index(t, c, s) >= NPH:
                            wait_used(dve, t, c, s)
                        nc.vector.tensor_tensor(p_lo[s % NPH][:, :], p_f[s % NPF][:, :], p_hi[s % NPH][:, :],
                                                ALU.subtract).then_inc(plo_dve, 1)
                    if s == 2 and is_block(t, c + 2):
                        queries(t, c + 2)
                    if s == 0 and not (isinstance(t, int) and NJ * t + c == 0):
                        context(t, c - 1)
                    if s in (3, 4) and not (isinstance(t, int) and NJ * t + c == 0):
                        add_context(t, c - 1, s - 3)
                    if s == STEPS - 1 and is_last(t):
                        transposed(c - 1)
                    if s == 5 and is_last(t):
                        dve.wait_ge(added, nth(t, c) * QT)
                        statistics(c - 1)
                    if s == 6 and is_last(t):
                        normalise(c - 1)

            def context(t, c):
                dve.wait_ge(ctx_ok, nth(t, c) + 1)
                nc.vector.tensor_tensor(ctx_lo[:, :], ctx_ps[0:CR, :], ctx_hi[:, :], ALU.subtract).then_inc(ctxlo_ok, 1)

            def transposed(j):
                dve.wait_ge(x1T_ok, j + 1)
                nc.vector.tensor_tensor(x1_lo[:, chunk(j)], misc[:, :], x1_hi[:, chunk(j)], ALU.subtract).then_inc(x1lo_ok, 1)

            def statistics(n):
                j = n % NJ
                for q in range(j * QT, (j + 1) * QT):
                    nc.vector.bn_stats(stats[:, q, :], resid[:, q, :]).then_inc(ln, 1)
                dve.wait_ge(ln, n * LN_ALL + QT)
                for q in range(j * QT, (j + 1) * QT):
                    nc.vector.bn_aggr(mv[:, q, :], stats[:, q, :]).then_inc(ln, 1)

            def normalise(n):
                j = n % NJ
                dve.wait_ge(pool_ln, 2 * n + 2)
                for q in range(j * QT, (j + 1) * QT):
                    nc.vector.tensor_scalar(resid[:, q, :], resid[:, q, :], mv[:, q, 0:1], rstd[:, q:q + 1],
                                            ALU.subtract, ALU.mult).then_inc(ln, 1)

            def result(j):
                tokens = resid[:, j * QT:(j + 1) * QT, :]
                dve.wait_ge(down_ok, j + 1)
                dve.wait_ge(ln, (j + 1) * LN_ALL)
                nc.vector.tensor_tensor(tokens, down_t(j).rearrange("p (q d) -> p q d", q=QT), tokens, ALU.add).then_inc(y_ok, 1)
                dve.wait_ge(y_ok, j + 1)
                statistics(NJ + j)
                normalise(NJ + j)

            blocks(dve, body)
            context(HEADS - 1, NJ - 1)
            for half in range(2):
                add_context(HEADS - 1, NJ - 1, half)
            dve.wait_ge(added, NB * QT)
            statistics(NJ - 1)
            normalise(NJ - 1)
            for j in range(NJ):
                if j == NJ - 1:
                    transposed(j)
                for k in range(HT):
                    dve.wait_ge(sil_ok, j * HT + k + 1)
                    dve.wait_ge(up_ok, j * HT + k + 1)
                    if j:
                        dve.wait_ge(hlo_ok, (j - 1) * HT + k + 1)
                    nc.vector.tensor_tensor(h_f[:, k, :], up_t(k), sil[:, k, :], ALU.mult).then_inc(h_ok, 1)
                if j:
                    result(j - 1)
            result(NJ - 1)

        @block.tensor
        def _(pe):
            pe.wait_ge(in_q, IN_Q)
            for h in range(HEADS):
                last = nc.tensor.matmul(misc[:, h * (R + 1):(h + 1) * (R + 1)],
                                        uq4_sb[:, h, :], ukb_sb[:, h, :],
                                        start=True, stop=True)
            last.then_inc(pe_w, 1)
            for h in range(HEADS):
                nc.tensor.matmul(ctx_ps[0:R, h:h + 1], ukb_sb[:, h, 0:R], buq_sb[:, h:h + 1], start=True, stop=True)
            pe.wait_ge(u_ok, 1)
            pe.wait_ge(const, CONST_ALL)
            nc.tensor.matmul(ctx_ps[:, HEADS:2 * HEADS], ones[:, :], ub[:, :], start=True, stop=True).then_inc(pe_w, 1)

            def latent_queries(c):
                nc.tensor.matmul(mscore[:, (c % 2) * QB:(c % 2 + 1) * QB], wlat_sb[:, 0, :], xT_sb[:, chunk(c)],
                                 start=True, stop=True).then_inc(pe_c, 1)

            pe.wait_ge(in_k, 16 * 2)
            for c in range(NJ):
                pe.wait_ge(in_t[c], 16)
                if c < 2:
                    latent_queries(c)
                nc.tensor.matmul(score[c // 2][:, (c % 2) * QB:(c % 2 + 1) * QB], wlat_sb[:, 1, :], xT_sb[:, chunk(c)],
                                 start=True, stop=True).then_inc(pe_k, 1)
            pe.wait_ge(dve_c, 2)
            for c in range(2, NJ):
                latent_queries(c)

            def project(t, c):
                if c % NJ == 0:
                    pe.wait_ge(wq_ok, head_of(t, c) * 2 + 2)
                nc.tensor.matmul(misc[:, :], wq_now[:, :], cq_hl[:, chunk(c % NJ)],
                                 start=True, stop=True).then_inc(proj_ok, 1)

            def half_unit(j, k, n, dst=mscore):
                qt = q_hl[j][:, (k // 2) * P:(k // 2 + 1) * P]
                keys = slice((k % 2) * HALF + n * QB, (k % 2) * HALF + (n + 1) * QB)
                o = dst[:, n * QB:(n + 1) * QB]
                nc.tensor.matmul(o, qt, k_hi2[:, keys], start=True, stop=False)
                nc.tensor.matmul(o, qt, k_lo2[:, keys], start=False, stop=True).then_inc(unit_ok, 1)

            def rows(t, c):
                pe.wait_ge(shift_ok, nth(t, c) + 1)
                for q in range(QT):
                    last = nc.tensor.matmul(misc[0:2, q * P:(q + 1) * P], shift_hl[:, q, :], ident_r[:, :],
                                            start=True, stop=True)
                last.then_inc(row_ok, 1)

            def scores(j, s):
                for a in range(2):
                    kt = slice((2 * s + a) * P, (2 * s + a + 1) * P)
                    o = score[s % 2][:, a * QB:(a + 1) * QB]
                    nc.tensor.matmul(o, k_hi2[:, kt], q_hl[j][:, :], start=True, stop=False)
                    last = nc.tensor.matmul(o, k_lo1[:, kt], q_hm[j][:, :], start=False, stop=True)
                last.then_inc(score_ok, 1)

            def contract(t, c, s):
                k = s % STEPS
                pe.wait_ge(phi_ok, nstep(t, c, s) + 1)
                for a in range(2):
                    last = nc.tensor.matmul(ctx_ps[:, :], vals[:, 2 * k + a, :], p_hi[k % NPH][:, a * QB:(a + 1) * QB],
                                            start=(k == 0 and a == 0), stop=False)
                last.then_inc(pvhi_ok, 1)

            def contract_lo(t, c, s):
                k = s % STEPS
                wait_lo(pe, t, c, s - 1)
                wait_lo(pe, t, c, s)
                for kk in (k - 1, k):
                    for a in range(2):
                        last = nc.tensor.matmul(ctx_ps[FEAT * a:FEAT * (a + 1), :], vals_b[:, 2 * kk + a, :],
                                                p_lo[kk % NPH][:, a * QB:(a + 1) * QB],
                                                start=False, stop=(kk == STEPS - 1))
                last.then_inc(pvlo_ok, 1)

            def project_context(t, c, half):
                hd = head_of(t, c)
                w_hi, w_lo = (w[:, hd, :] if isinstance(hd, int) else
                              w[:, bass.ds(hd, 1), :].rearrange("p a d -> p (a d)") for w in (wvo_hi, wvo_lo))
                for i in range(2):
                    q = slice((2 * half + i) * P, (2 * half + i + 1) * P)
                    o = outp[:, i, 0:OC]
                    nc.tensor.matmul(o, ctx_hi[:, q], w_hi, start=True, stop=False)
                    nc.tensor.matmul(o, ctx_hi[:, q], w_lo, start=False, stop=False)
                    last = nc.tensor.matmul(o, ctx_lo[:, q], w_hi, start=False, stop=True)
                last.then_inc(outp_ok, 1)

            def values(n):
                for t in range(n * KT // 2, (n + 1) * KT // 2):
                    o = (t % (KT // 2)) * 2 * R
                    nc.tensor.matmul(ctx_ps[:, o:o + R], k_hi2[0:R, t * P:(t + 1) * P], ident_r[0:R, 0:R],
                                     start=True, stop=True)
                    last = nc.tensor.matmul(ctx_ps[:, o + R:o + 2 * R], k_lo2[0:R, t * P:(t + 1) * P], ident_r[0:R, 0:R],
                                            start=True, stop=True)
                last.then_inc(pe_w, 1)

            def output_weights(n):
                for h in range(HH):
                    last = nc.tensor.matmul(ctx_ps[0:CR, h * D:(h + 1) * D], uv2_sb[:, n * HH + h, :],
                                            wo_sb[:, n * HH + h, :], start=True, stop=True)
                last.then_inc(pe_w, 1)

            pe.wait_ge(dve_c, 1)
            project(0, 0)
            pe.wait_ge(qlo_ok, 1)
            pe.wait_ge(dve_k, NJ)
            for n in range(AHEAD):
                if n == UNITS:
                    pe.wait_ge(qlo_ok, 2)
                if early[n] is mscore:
                    pe.wait_ge(dve_c, NJ)
                for i in range(2):
                    if n >= len(EARLY):
                        pe.wait_ge(unit_max, 2 * (n - len(EARLY)) + i + 1)
                    half_unit(n // UNITS, n % UNITS, i, early[n])
                if n == 0:
                    pe.wait_ge(act_w, 5)
                    values(0)
                if n == 2:
                    pe.wait_ge(dve_c, 2)
                    project(0, 1)
                if n == 3:
                    pe.wait_ge(act_w, 8)
                    values(1)
                    pe.wait_ge(in_v, 16 * 2)
                if n in (4, 5):
                    pe.wait_ge(act_w, 7 + n)
                    output_weights(n - 4)
                if n == 6:
                    pe.wait_ge(dve_c, NJ)
                    pe.wait_ge(act_w, 13)
                    for t in range(KT):
                        last = nc.tensor.matmul(ctx_ps[:, t * HEADS:(t + 1) * HEADS], cq_hl[:, t * P:(t + 1) * P], uw[:, :],
                                                start=True, stop=True)
                    last.then_inc(pe_w, 1)
            rows(0, 0)
            pe.wait_ge(row_in, 1)
            pe.wait_ge(lo1_ok, NJ)
            pe.wait_ge(unit_max, 2 * AHEAD)
            scores(0, 0)
            pe.wait_ge(u_ok, 2)

            def body(t, c):
                first = isinstance(t, int) and NJ * t + c == 0
                for s in range(STEPS):
                    k = s + AHEAD
                    if s == 2 and is_block(t, c + 2):
                        pe.wait_ge(row_in, nth(t, c) + 1)
                        project(t, c + 2)
                    if s == 6 and is_block(t, c + 1):
                        if first:
                            pe.wait_ge(qlo_ok, 3)
                        else:
                            pe.wait_ge(added, nth(t, c) * QT)
                        rows(t, c + 1)
                    if is_block(t, c + k // UNITS):
                        if k % UNITS == 0:
                            pe.wait_ge(qlo_ok, nth(t, c + k // UNITS) + 1)
                        for i in range(2):
                            pe.wait_ge(unit_max, nhalf(t, c, k, i) - 1)
                            half_unit((c + k // UNITS) % NJ, k % UNITS, i)
                    nxt = c + (s + 1) // STEPS
                    if is_block(t, nxt):
                        if s == STEPS - 1:
                            pe.wait_ge(row_in, nth(t, c + 1) + 1)
                        if not (first and s == 0):
                            pe.wait_ge(pf_ok, nstep(t, c, s))
                        scores(nxt % NJ, (s + 1) % STEPS)
                    if not (first and s == 0):
                        if s == 1 and not first:
                            pe.wait_ge(ctxlo_ok, nth(t, c))
                        cc = c - 1 if s == 0 else c
                        contract(t, cc, (s - 1) % STEPS)
                        if s in LO_AT:
                            contract_lo(t, cc, LO_AT[s])
                    if s in (3, 4) and not first:
                        if s == 3:
                            pe.wait_ge(ctxlo_ok, nth(t, c))
                            if first_use(t, c):
                                pe.wait_ge(wvo_ok, 2)
                            if is_last(t) and c >= 2:
                                pe.wait_ge(x1lo_ok, c - 1)
                            elif is_block(t, c + 2):
                                pe.wait_ge(qlo_ok, nth(t, c + 2) + 1)
                            else:
                                pe.wait_ge(row_in, nth(t, c) + 1)
                        else:
                            pe.wait_ge(added, nth(t, c - 1) * QT + 2)
                        project_context(t, c - 1, s - 3)
                    if s == STEPS - 1 and is_last(t):
                        if is_block(t, c + 1):
                            pe.wait_ge(row_in, nth(t, c) + 2)
                        transpose(c - 1)

            def transpose(j):
                pe.wait_ge(ln, (j + 1) * LN_ALL)
                for q in range(QT):
                    last = nc.tensor.transpose(misc[:, q * P:(q + 1) * P], resid[:, j * QT + q, :], ident[:, :])
                last.then_inc(x1T_ps, 1)

            blocks(pe, body)
            contract(HEADS - 1, NJ - 1, STEPS - 1)
            contract_lo(HEADS - 1, NJ - 1, STEPS - 1)
            pe.wait_ge(x1lo_ok, NJ - 1)
            pe.wait_ge(ctxlo_ok, NB)
            project_context(HEADS - 1, NJ - 1, 0)
            pe.wait_ge(added, (NB - 1) * QT + 2)
            project_context(HEADS - 1, NJ - 1, 1)

            pe.wait_ge(ffw_ok, 3)
            pe.wait_ge(pf_ok, NB * STEPS)

            def gate_up(j):
                pe.wait_ge(x1lo_ok, j + 1)
                for k in range(HT):
                    if j:
                        pe.wait_ge(h_ok, (j - 1) * HT + k + 1)
                    for off, dst, done in ((0, gate_t(k), gate_ok), (H, up_t(k), up_ok)):
                        w = slice(off + k * P, off + (k + 1) * P)
                        nc.tensor.matmul(dst, wf_hi[:, w], x1_hi[:, chunk(j)], start=True, stop=False)
                        nc.tensor.matmul(dst, wf_lo[:, w], x1_hi[:, chunk(j)], start=False, stop=False)
                        nc.tensor.matmul(dst, wf_hi[:, w], x1_lo[:, chunk(j)], start=False, stop=True).then_inc(done, 1)

            def down(j):
                pe.wait_ge(hlo_ok, j * HT + HT)
                if j:
                    pe.wait_ge(y_ok, j)
                for q in range(QT):
                    tok = slice(q * P, (q + 1) * P)
                    o = down_t(j)[:, q * D:(q + 1) * D]
                    for k in range(HT):
                        w = slice(2 * H + k * D, 2 * H + (k + 1) * D)
                        nc.tensor.matmul(o, h_hi[j % 2][:, k, tok], wf_hi[:, w], start=(k == 0), stop=False)
                        nc.tensor.matmul(o, h_hi[j % 2][:, k, tok], wf_lo[:, w], start=False, stop=False)
                        last = nc.tensor.matmul(o, h_lo[j % 2][:, k, tok], wf_hi[:, w], start=False, stop=(k == HT - 1))
                last.then_inc(down_ok, 1)

            for j in range(NJ):
                if j == NJ - 1:
                    transpose(j)
                gate_up(j)
                if j:
                    down(j - 1)
            down(NJ - 1)


def kernel(**inputs):
    import concourse.bacc as bacc
    from concourse.bass_utils import run_bass_kernel_spmd

    a = {n.replace("L0_attn_", "").replace("L0_ffn_", ""): np.asarray(v) for n, v in inputs.items()}
    b, s, d = a["h_t"].shape
    r = a["W_DKV"].shape[1]
    heads = a["b_QR"].shape[0] // r
    dk = a["W_UK"].shape[1] // heads
    ht = a["w_down"].shape[1] // d

    def cat(*parts):
        return np.concatenate(parts, axis=-1)

    def by_head(w):
        return w.reshape(r, heads, dk).transpose(2, 1, 0)

    def bias(v):
        return v.reshape(heads, dk).T[:, :, None]

    x = a["h_t"].reshape(s, d)
    gap = np.zeros((r, heads), x.dtype)
    laid = {
        "x": x,
        "xT": x.T,
        "wlat": np.stack([cat(*[a["W_DQ"]] * 4), cat(a["W_DKV"], a["W_KR"], a["W_DKV"], a["W_KR"])], axis=1),
        "blat": np.stack([cat(*[a["b_DQ"]] * 4), cat(a["b_DKV"], a["b_KR"], a["b_DKV"], a["b_KR"])], axis=1),
        "uq4": cat(*[by_head(a["W_UQ"])] * 4),
        "ukb": cat(by_head(a["W_UK"]), bias(a["b_UK"])),
        "buq": a["b_UQ"].reshape(heads, dk).T,
        "wqr4": np.concatenate([a["W_QR"].reshape(r, heads, r)] * 4),
        "qb0": np.concatenate([gap, a["b_QR"].reshape(heads, r).T] * 2),
        "uv2": cat(by_head(a["W_UV"]), bias(a["b_UV"]), np.zeros((dk, heads, r - 1), x.dtype),
                   by_head(a["W_UV"]), bias(a["b_UV"])),
        "wo": a["W_O"].reshape(heads, dk, d).transpose(1, 0, 2),
        "bo": a["b_O"],
        "wg": a["w_gate"].T,
        "wu": a["w_up"].T,
        "wd": a["w_down"].T.reshape(ht, d, d).transpose(1, 0, 2),
    }
    nc = bacc.Bacc("TRN2", target_bir_lowering=False, num_devices=1)
    arrays, args = {}, []
    for n, v in laid.items():
        arrays[f"in_{n}"] = np.ascontiguousarray(v)
        args.append(nc.dram_tensor(f"in_{n}", v.shape, mybir.dt.from_np(v.dtype), kind="ExternalInput").ap())
    args.append(nc.dram_tensor("out_0", (s, d), F32, kind="ExternalOutput").ap())
    attention_ffn(nc, *args)
    res = run_bass_kernel_spmd(nc, [arrays], core_ids=[0])
    return res.results[0]["out_0"].reshape(b, s, d)
```

```python
import numpy as np
import concourse.bass as bass
from concourse import mybir
from contextlib import ExitStack

F32 = mybir.dt.float32
F32R = mybir.dt.float32r
I32 = mybir.dt.int32
BF16 = mybir.dt.bfloat16
ALU = mybir.AluOpType
ACT = mybir.ActivationFunctionType
AX = mybir.AxisListType


def attention_ffn(nc, x, xT, latw, qw, wqr4, vw, bo, ffw, out, HEADS):
    P = 128
    S = x.shape[0]
    D = x.shape[1]
    R = wqr4.shape[2]
    FEAT = 2 * R
    QB = 512
    NJ = S // QB
    NB = HEADS * NJ
    QT = QB // P
    KT = S // P
    STEPS = KT // 2
    HALF = S // 2
    UNITS = 2 * QT
    AHEAD = UNITS + 3
    LO_AT = {3: 1, 5: 3, 7: 5, 0: 7}
    POOL_STEPS = (3, 4, 5)
    HI, SUM, LO, SUM2 = 0, R, 2 * R, 3 * R
    CR = SUM2 + 1
    DEN = D
    OC = D + 2
    H = ffw.shape[1] // 3
    HT = H // P
    SCALE = 1.0 / float(np.sqrt(P + R))
    WSCALE = float(np.float32(1.0 / 127.0))
    EPS = 1e-5
    assert UNITS == STEPS and D == P and x.shape[1] == P

    ctx = ExitStack()
    with ctx:
        def sb(name, shape, dt=F32):
            return ctx.enter_context(nc.sbuf_tensor(name, shape, dt))

        def ps(name, shape):
            return ctx.enter_context(nc.psum_tensor(name, shape, F32))

        def sem(name):
            return ctx.enter_context(nc.semaphore(name))

        xT_sb = sb("xT_sb", [P, S])
        resid = sb("resid", [P, KT, D])
        bo_sb = sb("bo_sb", [P, D])
        def views(t, *shapes):
            at, out = 0, []
            for sh in shapes:
                n = int(np.prod(sh))
                v = t[:, at:at + n]
                out.append(v if len(sh) == 1 else v.rearrange("p (a b) -> p a b", a=sh[0]))
                at += n
            return out

        latw_sb = sb("latw_sb", list(latw.shape))
        wlat_sb, blat_sb = views(latw_sb, (2, 4 * R),
                                 (2,))
        qw_sb = sb("qw_sb", list(qw.shape))
        uq4_sb, ukb_sb, buq_sb, qbias = views(
            qw_sb, (HEADS, 4 * R),
            (HEADS, R + 1),
            (HEADS,),
            (HEADS,))
        vw_sb = sb("vw_sb", list(vw.shape))
        uv2_sb, wo_sb = views(vw_sb, (HEADS, CR),
                              (HEADS, D))
        wint = sb("wint", [P, 2 * H + HT * D], I32)
        wffn = sb("wffn", [P, 2 * H + HT * D])
        wf_hl = sb("wf_hl", [P, 2, 2 * H + HT * D], F32R)
        wf_hi, wf_lo = wf_hl[:, 0], wf_hl[:, 1]

        ident = sb("ident", [P, P])
        ident_r = sb("ident_r", [P, P], F32R)
        ones = sb("ones", [P, P])
        mhalf = sb("mhalf", [P, KT])

        k_hi2 = sb("k_hi2", [P, S], F32R)
        k_lo2 = sb("k_lo2", [P, S], F32R)
        k_lo1 = sb("k_lo1", [FEAT + 2, S], F32R)
        cq_hl = sb("cq_hl", [P, S], F32R)
        vals = sb("vals", [P, KT, P], F32R)
        vals_b = sb("vals_b", [P, KT, FEAT], BF16)
        wqf = sb("wqf", [P, HEADS, FEAT])
        wq = sb("wq", [P, HEADS, FEAT], F32R)
        wq_now = sb("wq_now", [P, 2 * FEAT], F32R)
        qb_now = sb("qb_now", [P, 1])
        uwf = sb("uwf", [P, HEADS])
        uw = sb("uw", [P, HEADS], F32R)
        uconst = sb("uconst", [P, HEADS])
        u = sb("u", [P, HEADS * KT])
        ub = sb("ub", [P, HEADS])
        wvof = sb("wvof", [CR, HEADS, OC])
        wvo_hi = sb("wvo_hi", [CR, HEADS, OC], F32R)
        wvo_lo = sb("wvo_lo", [CR, HEADS, OC], F32R)

        q_hl = [sb(f"q_hl{j}", [P, QB], F32R) for j in range(NJ)]
        q_hm = [sb(f"q_hm{j}", [FEAT + 2, QB], F32R) for j in range(NJ)]
        mx_part = [sb(f"mx_part{j}", [P, QT, 4]) for j in range(2)]
        mx = sb("mx", [P, QT])
        mxu = sb("mxu", [P, QT])
        shift = sb("shift", [P, QT])
        shift_hl = sb("shift_hl", [P, QT, 2], F32R)
        NPH = 4
        p_hi = [sb(f"p_hi{n}", [P, 2 * QB], F32R) for n in range(NPH)]
        p_lo = [sb(f"p_lo{n}", [P, 2 * QB], BF16) for n in range(NPH)]
        NPF = 4
        p_f = [sb(f"p_f{n}", [P, 2 * QB]) for n in range(NPF)]
        ctx_low = sb("ctx_low", [R + 1, QB])
        ctx_f = sb("ctx_f", [R + 1, QB])
        ctx_hl = sb("ctx_hl", [CR, QB], F32R)
        rden = sb("rden", [P, QT])

        score = [ps(f"score{n}", [P, 2 * QB]) for n in range(2)]
        mscore = ps("mscore", [P, HALF])
        ctx_ps = ps("ctx_ps", [P, QB])
        misc = ps("misc", [P, QB])
        outp = misc[:, :].rearrange("p (t c) -> p t c", t=2)

        stats = sb("stats", [P, KT, 6])
        mv = sb("mv", [P, KT, 2])
        veps = sb("veps", [P, KT])
        rstd = sb("rstd", [P, KT])
        x1_hi = cq_hl
        x1_lo = sb("x1_lo", [P, S], F32R)
        h_f = sb("h_f", [P, HT, QB])
        hidden_hi = (k_hi2, k_lo2)
        h_hi = [t[:, 0:HT * QB].rearrange("p (k q) -> p k q", k=HT) for t in hidden_hi]
        h_lo_sb = sb("h_lo_sb", [P, 2, HT, QB], F32R)
        h_lo = [h_lo_sb[:, n] for n in range(2)]
        sil = sb("sil", [P, HT, QB])

        in_k = sem("in_k")
        in_t = [sem(f"in_t{c}") for c in range(NJ)]
        in_q = sem("in_q")
        in_r = sem("in_r")
        in_v = sem("in_v")
        in_x = sem("in_x")
        in_f = sem("in_f")
        const = sem("const")
        ident_ok = sem("ident_ok")
        filled = sem("filled")
        pool_r = sem("pool_r")
        pe_k = sem("pe_k")
        act_k = sem("act_k")
        dve_k = sem("dve_k")
        lo1_ok = sem("lo1_ok")
        pe_c = sem("pe_c")
        act_c = sem("act_c")
        dve_c = sem("dve_c")
        pe_w = sem("pe_w")
        act_w = sem("act_w")
        dve_w = sem("dve_w")
        u_ok = sem("u_ok")
        wvo_ok = sem("wvo_ok")
        wq_ok = sem("wq_ok")
        proj_ok = sem("proj_ok")
        qhi_ok = sem("qhi_ok")
        qlo_ok = sem("qlo_ok")
        unit_ok = sem("unit_ok")
        unit_max = sem("unit_max")
        mchain = sem("mchain")
        shift_ok = sem("shift_ok")
        row_ok = sem("row_ok")
        row_in = sem("row_in")
        score_ok = sem("score_ok")
        phi_ok = sem("phi_ok")
        pf_ok = sem("pf_ok")
        plo_dve = sem("plo_dve")
        plo_pool = sem("plo_pool")
        pvhi_ok = sem("pvhi_ok")
        pvlo_ok = sem("pvlo_ok")
        ctx_ok = sem("ctx_ok")
        ctxsum_ok = sem("ctxsum_ok")
        ctxhi_ok = sem("ctxhi_ok")
        ctxlo_ok = sem("ctxlo_ok")
        outp_ok = sem("outp_ok")
        den_ok = sem("den_ok")
        added = sem("added")
        ffw_ok = sem("ffw_ok")
        ln = sem("ln")
        pool_ln = sem("pool_ln")
        x1T_ps = sem("x1T_ps")
        x1T_ok = sem("x1T_ok")
        x1lo_ok = sem("x1lo_ok")
        gate_ok = sem("gate_ok")
        up_ok = sem("up_ok")
        sil_ok = sem("sil_ok")
        h_ok = sem("h_ok")
        hhi_ok = sem("hhi_ok")
        hlo_ok = sem("hlo_ok")
        hlo_last = sem("hlo_last")
        down_ok = sem("down_ok")
        y_hi = sem("y_hi")
        y_ok = sem("y_ok")
        out_ok = sem("out_ok")

        block = ctx.enter_context(nc.Block())
        resid_v = x.rearrange("(t p) d -> p t d", p=P)
        out_v = out.rearrange("(t p) d -> p t d", p=P)

        def chunk(c):
            return slice(c * QB, (c + 1) * QB)

        def blocks(eng, body):
            body(0, 0)
            with eng.Fori(0, HEADS - 1) as t:
                for c in range(1, NJ + 1):
                    body(t, c)
            for c in range(NB - NJ + 1, NB):
                body(HEADS - 1, c - NB + NJ)

        def is_block(t, c):
            return not isinstance(t, int) or 0 <= NJ * t + c < NB

        def is_first(t, c):
            return isinstance(t, int) and NJ * t + c == 0

        def is_last(t):
            return isinstance(t, int) and t == HEADS - 1

        def nth(t, c):
            return t * NJ + c

        def nstep(t, c, s):
            return t * (NJ * STEPS) + (c * STEPS + s)

        def nhalf(t, c, k, i):
            return t * (NJ * UNITS * 2) + ((c * UNITS + k) * 2 + i)

        def wait_lo(eng, t, c, s):
            c, s = c + s // STEPS, s % STEPS
            pool = len([k for k in POOL_STEPS if k <= s])
            n = len(POOL_STEPS)
            if s in POOL_STEPS:
                eng.wait_ge(plo_pool, t * (NJ * n) + (c * n + pool))
            else:
                n = STEPS - n
                eng.wait_ge(plo_dve, t * (NJ * n) + (c * n + s + 1 - pool))

        def wait_used(eng, t, c, s):
            eng.wait_ge(pvlo_ok, t * (NJ * STEPS // 2) + (c * STEPS + s - NPH) // 2 + 1)

        def first_use(t, c):
            return c == 1 and not isinstance(t, int)

        def step_index(t, c, s):
            return NJ * STEPS * t + c * STEPS + s if isinstance(t, int) else STEPS * NJ

        def head_of(t, c):
            return t + c // NJ

        def gate_t(k):
            return (score[0][:, 0:QB], score[0][:, QB:2 * QB], score[1][:, 0:QB])[k]

        def up_t(k):
            return (score[1][:, QB:2 * QB], mscore[:, 0:QB], mscore[:, QB:2 * QB])[k]

        def down_t(q):
            return (ctx_ps, misc)[q // 2][:, (q % 2) * 2 * D:(q % 2 + 1) * 2 * D].rearrange("p (n d) -> p n d", n=2)

        EARLY = (0, 1, 2, 0, 1, 2, 0, 1, 2, 1, 2)
        early = [(score[0], score[1], mscore)[n] for n in EARLY]
        assert len(EARLY) == AHEAD

        def early_before(n):
            return max([m for m in range(n) if EARLY[m] == EARLY[n]], default=None)

        WARM, WARM_SPLIT, WARM_HIDDEN = 8, 10, 10
        NORM_AT = 1
        CTX_HI_AT = 1
        LAST_IN = (2, 1)
        HH = HEADS // 2
        DVE_W_ALL = 6
        ACT_W_ALL = 13
        CONST_ALL = 12

        LN_VAR = 2 * QT
        LN_ALL = LN_VAR + QT

        @block.sync
        def _(sp):
            sp.dma_start(latw_sb[:, :], latw).then_inc(in_k, 16)
            for c in range(NJ):
                sp.dma_start(xT_sb[:, chunk(c)], xT[:, chunk(c)]).then_inc(in_t[c], 16)
                if c == 1:
                    sp.dma_start(qw_sb[:, :], qw).then_inc(in_q, 16)
                    sp.dma_start(wqf[:, :, R:FEAT], wqr4).then_inc(in_r, 16)
            sp.dma_start(resid[:, :, :], resid_v).then_inc(in_x, 16)
            sp.dma_start(bo_sb[:, :], bo.partition_broadcast(P)).then_inc(in_x, 16)
            sp.dma_start(wint[:, :], ffw).then_inc(in_f, 16)
            sp.dma_start(vw_sb[:, :], vw).then_inc(in_v, 16)
            for j in range(NJ):
                sp.wait_ge(ln, (NJ + j + 1) * LN_ALL)
                sp.dma_start(out_v[:, j * QT:(j + 1) * QT, :], resid[:, j * QT:(j + 1) * QT, :]).then_inc(out_ok, 16)
            sp.wait_ge(out_ok, 16 * NJ)

        @block.gpsimd
        def _(pool):
            nc.gpsimd.memset(ones[:, :], 1.0).then_inc(const, 1)
            nc.gpsimd.memset(ident[:, :], 0.0).then_inc(const, 1)
            nc.gpsimd.memset(mhalf[:, :], -0.5).then_inc(const, 1)
            nc.gpsimd.memset(vals[:, :, SUM:LO].bitcast(F32), 0.0).then_inc(const, 1)
            nc.gpsimd.memset(vals[:, :, SUM2:P].bitcast(F32), 0.0).then_inc(const, 1)
            nc.gpsimd.memset(vals_b[:, :, SUM:FEAT], 0.0).then_inc(const, 1)
            nc.gpsimd.memset(wvof[:, :, D:OC], 0.0).then_inc(const, 1)
            pool.wait_ge(const, 7)
            nc.gpsimd.memset(vals[:, :, SUM:SUM + 1].bitcast(F32), 1.0).then_inc(const, 1)
            nc.gpsimd.memset(vals_b[:, :, SUM:SUM + 1], 1.0).then_inc(const, 1)
            pool.wait_ge(const, 9)
            nc.gpsimd.memset(wvof[SUM:SUM + 1, :, DEN:DEN + 1], 1.0).then_inc(const, 1)
            pool.wait_ge(const, 10)
            nc.gpsimd.memset(wvof[SUM2:CR, :, DEN:DEN + 1], 1.0).then_inc(const, 1)
            pool.wait_ge(const, 11)
            nc.gpsimd.affine_select(out=ident[:, :], in_=ident[:, :], compare_op=ALU.not_equal, fill=1.0,
                                    base=0, pattern=[[-1, P]], channel_multiplier=1).then_inc(const, 1)
            def twice(t):
                return t[:, :].rearrange("p (n c) -> p n c", n=2)

            pool.wait_ge(dve_w, DVE_W_ALL)
            nc.gpsimd.tensor_copy(twice(wq_now), wq[:, 0:1, :].to_broadcast([P, 2, FEAT])).then_inc(wq_ok, 1)
            pool.wait_ge(act_w, 5)
            pool.wait_ge(in_q, 16)
            nc.gpsimd.tensor_copy(qb_now[:, :], qbias[:, 0:1]).then_inc(wq_ok, 1)
            pool.wait_ge(in_x, 32)
            nc.gpsimd.tensor_tensor(resid[:, :, :], resid[:, :, :],
                                    bo_sb[:, :].unsqueeze(1).to_broadcast([P, KT, D]), ALU.add).then_inc(pool_r, 1)
            pool.wait_ge(in_f, 16)
            nc.gpsimd.tensor_scalar(wffn[:, :], wint[:, :], WSCALE, None, ALU.mult).then_inc(ffw_ok, 1)
            pool.wait_ge(ffw_ok, 1)
            nc.gpsimd.tensor_copy(wf_hi[:, :], wffn[:, :]).then_inc(ffw_ok, 1)
            pool.wait_ge(ffw_ok, 2)
            nc.gpsimd.tensor_tensor(wf_lo[:, :], wffn[:, :], wf_hi[:, :], ALU.subtract).then_inc(ffw_ok, 1)

            def rsqrt(n):
                cols = slice((n % NJ) * QT, (n % NJ + 1) * QT)
                pool.wait_ge(ln, n * LN_ALL + LN_VAR)
                nc.gpsimd.tensor_scalar(veps[:, cols], mv[:, cols, 1], EPS, None, ALU.add).then_inc(pool_ln, 1)
                pool.wait_ge(pool_ln, 2 * n + 1)
                nc.gpsimd.tensor_tensor(rstd[:, cols], veps[:, cols], mhalf[:, cols], ALU.pow).then_inc(pool_ln, 1)

            def context_lo(t, c):
                pool.wait_ge(ctxhi_ok, nth(t, c) + 1)
                pool.wait_ge(plo_pool, (len(POOL_STEPS) * NJ) * t + len(POOL_STEPS) * (c + 1))
                if c == 0:
                    pool.wait_ge(wvo_ok, 2)
                elif c == 1 and not isinstance(t, int):
                    pool.wait_ge(wq_ok, t * 2 + 4)
                elif is_last(t) and c > 0:
                    pool.wait_ge(pool_ln, 2 * c)
                nc.gpsimd.tensor_tensor(ctx_hl[LO:CR, :], ctx_f[:, :], ctx_hl[0:R + 1, :], ALU.subtract).then_inc(ctxlo_ok, 1)

            def body(t, c):
                for s in range(STEPS):
                    if s == CTX_HI_AT + 1 and not is_first(t, c):
                        context_lo(t, c - 1)
                    if s == POOL_STEPS[0] and not is_first(t, c):
                        pool.wait_ge(ctxlo_ok, nth(t, c))
                    if s in POOL_STEPS:
                        pool.wait_ge(pf_ok, nstep(t, c, s) + 1)
                        if step_index(t, c, s) >= NPH:
                            wait_used(pool, t, c, s)
                        nc.gpsimd.tensor_tensor(p_lo[s % NPH][:, :], p_f[s % NPF][:, :], p_hi[s % NPH][:, :],
                                                ALU.subtract).then_inc(plo_pool, 1)
                    if s == STEPS - 2 and is_first(t, c):
                        pool.wait_ge(act_w, ACT_W_ALL)
                        nc.gpsimd.tensor_copy(wvo_hi[:, :, :], wvof[:, :, :]).then_inc(wvo_ok, 1)
                        pool.wait_ge(wvo_ok, 1)
                        nc.gpsimd.tensor_tensor(wvo_lo[:, :, :], wvof[:, :, :], wvo_hi[:, :, :],
                                                ALU.subtract).then_inc(wvo_ok, 1)
                    if s == STEPS - 2 and c == 1 and not isinstance(t, int):
                        pool.wait_ge(qlo_ok, t * NJ + NJ)
                        nc.gpsimd.tensor_copy(twice(wq_now),
                                              wq[:, bass.ds(t + 1, 1), :].to_broadcast([P, 2, FEAT])).then_inc(wq_ok, 1)
                        nc.gpsimd.tensor_copy(qb_now[:, :], qbias[:, bass.ds(t + 1, 1)]).then_inc(wq_ok, 1)
                    if s == STEPS - 2 and is_last(t):
                        rsqrt(c - 1)

            blocks(pool, body)
            context_lo(HEADS - 1, NJ - 1)
            pool.wait_ge(ctxlo_ok, NB)
            for j in range(NJ):
                for k in range(HT):
                    if (j, k) == (NJ - 1, HT - 1):
                        break
                    pool.wait_ge(hhi_ok, j * HT + k + 1)
                    if j >= 2:
                        pool.wait_ge(down_ok, 2 * (j - 1))
                    nc.gpsimd.tensor_tensor(h_lo[j % 2][:, k, :], h_f[:, k, :], h_hi[j % 2][:, k, :],
                                            ALU.subtract).then_inc(hlo_ok, 1)
                rsqrt(NJ + j - 1)
            rsqrt(2 * NJ - 1)

        @block.scalar
        def _(act):
            act.wait_ge(const, CONST_ALL)
            nc.scalar.activation(ident_r[:, :], ident[:, :], ACT.Identity).then_inc(ident_ok, 1)
            act.wait_ge(in_k, 16)

            def keys(c):
                act.wait_ge(pe_k, c + 1)
                src = score[c // 2][:, (c % 2) * QB:(c % 2 + 1) * QB]
                nc.scalar.activation(k_hi2[:, chunk(c)], src, ACT.Identity, bias=blat_sb[:, 1:2]).then_inc(act_k, 1)

            def latent_queries(c):
                act.wait_ge(pe_c, c + 1)
                src = mscore[:, (c % 2) * QB:(c % 2 + 1) * QB]
                nc.scalar.activation(cq_hl[:, chunk(c)], src, ACT.Identity, bias=blat_sb[:, 0:1]).then_inc(act_c, 1)

            for c in range(NJ):
                if c < 2:
                    latent_queries(c)
                if c == 2:
                    act.wait_ge(pe_w, 1)
                    wqp = misc[:, 0:HEADS * (R + 1)].rearrange("p (h c) -> p h c", h=HEADS)
                    nc.scalar.copy(wqf[:, :, 0:R], wqp[:, :, 0:R]).then_inc(act_w, 1)
                    nc.scalar.copy(uwf[:, :], wqp[:, :, R]).then_inc(act_w, 1)
                    act.wait_ge(pe_w, 2)
                    act.wait_ge(in_q, 16)
                    for r in range(2):
                        nc.scalar.copy(qbias[FEAT * r:FEAT * r + R, :], ctx_ps[0:R, 0:HEADS]).then_inc(act_w, 1)
                    nc.scalar.copy(uconst[:, :], ctx_ps[:, HEADS:2 * HEADS]).then_inc(act_w, 1)
                keys(c)

            def queries(t, c):
                j = c % NJ
                act.wait_ge(proj_ok, nth(t, c) + 1)
                nc.scalar.activation(q_hl[j][:, :], misc[:, :], ACT.Identity, bias=qb_now[:, 0:1]).then_inc(qhi_ok, 1)
                nc.scalar.activation(q_hm[j][0:FEAT, :], misc[0:FEAT, :], ACT.Identity, bias=qb_now[0:FEAT, 0:1]).then_inc(qhi_ok, 1)

            def shift_row(t, c):
                act.wait_ge(row_ok, nth(t, c) + 1)
                nc.scalar.copy(q_hm[c % NJ][FEAT:FEAT + 2, :], misc[0:2, :]).then_inc(row_in, 1)

            def context(t, c):
                act.wait_ge(pvlo_ok, t * (NJ * STEPS // 2) + (c + 1) * (STEPS // 2))
                nc.scalar.copy(ctx_low[:, :], ctx_ps[LO:CR, :]).then_inc(ctx_ok, 1)

            def context_hi(t, c):
                act.wait_ge(ctxsum_ok, nth(t, c) + 1)
                nc.scalar.copy(ctx_hl[0:R + 1, :], ctx_f[:, :]).then_inc(ctxhi_ok, 1)

            latent_queries(2)
            queries(0, 0)
            latent_queries(3)
            for n in range(2):
                if n == 1:
                    queries(0, 1)
                act.wait_ge(pe_w, 3 + n)
                vp = ctx_ps[:, :].rearrange("p (t c) -> p t c", t=KT // 2)
                kt = slice(n * KT // 2, (n + 1) * KT // 2)
                nc.scalar.copy(vals[:, kt, HI:HI + R], vp[:, :, 0:R]).then_inc(act_w, 1)
                nc.scalar.copy(vals[:, kt, LO:LO + R], vp[:, :, R:2 * R]).then_inc(act_w, 1)
                nc.scalar.copy(vals_b[:, kt, 0:R], vp[:, :, 0:R]).then_inc(act_w, 1)
            act.wait_ge(dve_k, NJ)
            for c in range(NJ):
                nc.scalar.copy(k_lo1[0:FEAT, chunk(c)], k_lo2[0:FEAT, chunk(c)]).then_inc(lo1_ok, 1)
            shift_row(0, 0)

            def output_weights(n):
                act.wait_ge(pe_w, 6 + n)
                nc.scalar.copy(wvof[:, n * HH:(n + 1) * HH, 0:D],
                               misc[0:CR, :].rearrange("p (h d) -> p h d", h=HH)).then_inc(act_w, 1)

            def body(t, c):
                for s in range(STEPS):
                    if s == 1 and not is_first(t, c):
                        context(t, c - 1)
                    act.wait_ge(score_ok, nstep(t, c, s) + 1)
                    if step_index(t, c, s) >= NPH:
                        act.wait_ge(pvhi_ok, nstep(t, c, s) - (NPH - 1))
                        wait_lo(act, t, c, s - NPH)
                    nc.scalar.activation(p_hi[s % NPH][:, :], score[s % 2][:, :], ACT.Exp, scale=SCALE).then_inc(phi_ok, 1)
                    nc.scalar.activation(p_f[s % NPF][:, :], score[s % 2][:, :], ACT.Exp, scale=SCALE).then_inc(pf_ok, 1)
                    if s == CTX_HI_AT and not is_first(t, c):
                        context_hi(t, c - 1)
                    if s == 2 and is_block(t, c + 2):
                        queries(t, c + 2)
                    if s in (3, 4) and is_first(t, c):
                        output_weights(s - 3)
                    if s == 6 and is_block(t, c + 1):
                        shift_row(t, c + 1)
                    if s == STEPS - 1 and is_last(t):
                        transposed(c - 1)

            def transposed(j):
                act.wait_ge(x1T_ps, j + 1)
                nc.scalar.copy(x1_hi[:, chunk(j)], misc[:, :]).then_inc(x1T_ok, 1)

            blocks(act, body)
            context(HEADS - 1, NJ - 1)
            context_hi(HEADS - 1, NJ - 1)

            for j in range(NJ):
                for k in range(HT):
                    if (j, k) == LAST_IN:
                        transposed(NJ - 1)
                    act.wait_ge(gate_ok, j * HT + k + 1)
                    nc.scalar.activation(sil[:, k, :], gate_t(k), ACT.Silu).then_inc(sil_ok, 1)
                for k in range(HT):
                    act.wait_ge(h_ok, j * HT + k + 1)
                    if j >= 2:
                        act.wait_ge(down_ok, 2 * (j - 1))
                    nc.scalar.copy(h_hi[j % 2][:, k, :], h_f[:, k, :]).then_inc(hhi_ok, 1)

        @block.vector
        def _(dve):
            dve.wait_ge(const, CONST_ALL)
            nc.vector.memset(k_lo1[FEAT:FEAT + 2, :].bitcast(F32), 1.0).then_inc(filled, 1)
            nc.vector.memset(ctx_hl[SUM:LO, :].bitcast(F32), 0.0).then_inc(filled, 1)
            lo = slice(FEAT, 2 * FEAT)

            def keys(c):
                dve.wait_ge(act_k, c + 1)
                src = score[c // 2][:, (c % 2) * QB:(c % 2 + 1) * QB]
                nc.vector.scalar_tensor_tensor(out=k_lo2[:, chunk(c)], in0=src, scalar=blat_sb[:, 1:2],
                                               in1=k_hi2[:, chunk(c)], op0=ALU.add, op1=ALU.subtract).then_inc(dve_k, 1)

            def latent_queries(c):
                dve.wait_ge(act_c, c + 1)
                src = mscore[:, (c % 2) * QB:(c % 2 + 1) * QB]
                nc.vector.scalar_tensor_tensor(out=cq_hl[lo, chunk(c)], in0=src[lo, :], scalar=blat_sb[lo, 0:1],
                                               in1=cq_hl[lo, chunk(c)], op0=ALU.add, op1=ALU.subtract).then_inc(dve_c, 1)

            dve.wait_ge(in_k, 16)
            for c in range(NJ):
                if c < 2:
                    latent_queries(c)
                if c == 1:
                    dve.wait_ge(in_q, 16)
                    nc.vector.tensor_tensor(ub[:, :], buq_sb[:, :], ukb_sb[:, :, R], ALU.mult).then_inc(u_ok, 1)
                if c == 2:
                    dve.wait_ge(act_w, 2)
                    dve.wait_ge(in_r, 16)
                    nc.vector.tensor_copy(wq[:, :, :], wqf[:, :, :]).then_inc(dve_w, 1)
                    nc.vector.tensor_copy(uw[:, :], uwf[:, :]).then_inc(dve_w, 1)
                    dve.wait_ge(dve_w, 2)
                    for r in (1, 3):
                        part = slice(R * r, R * (r + 1))
                        nc.vector.tensor_tensor(wq[part, :, :], wqf[part, :, :], wq[part, :, :], ALU.subtract).then_inc(dve_w, 1)
                        nc.vector.tensor_tensor(uw[part, :], uwf[part, :], uw[part, :], ALU.subtract).then_inc(dve_w, 1)
                keys(c)

            def queries(t, c):
                j = c % NJ
                dve.wait_ge(qhi_ok, nth(t, c) * 2 + 2)
                nc.vector.scalar_tensor_tensor(out=q_hl[j][lo, :], in0=misc[lo, :], scalar=qb_now[lo, 0:1], in1=q_hl[j][lo, :],
                                               op0=ALU.add, op1=ALU.subtract).then_inc(qlo_ok, 1)

            def unit(t, c, k, src=mscore):
                for i in range(2):
                    col = (k % 2) * 2 + i
                    dve.wait_ge(unit_ok, nhalf(t, c, k, i) + 1)
                    nc.vector.reduce_max(mx_part[(c + k // UNITS) % 2][:, k % UNITS // 2, col:col + 1],
                                         src[:, i * QB:(i + 1) * QB], AX.X).then_inc(unit_max, 1)

            def shifts(t, c):
                j, b = c % NJ, nth(t, c)
                off = head_of(t, c) * KT + j * QT
                uj = u[:, off:off + QT] if isinstance(off, int) else u[:, bass.ds(off, QT)]
                dve.wait_ge(unit_max, nhalf(t, c, UNITS, 0))
                nc.vector.reduce_max(mx[:, :], mx_part[c % 2][:, :, :], AX.X).then_inc(mchain, 1)
                dve.wait_ge(mchain, b * 4 + 1)
                nc.vector.tensor_tensor(mxu[:, :], mx[:, :], uj, ALU.add).then_inc(mchain, 1)
                dve.wait_ge(mchain, b * 4 + 2)
                nc.vector.tensor_tensor(shift[:, :], uj, mxu[:, :], ALU.subtract).then_inc(mchain, 1)
                dve.wait_ge(mchain, b * 4 + 3)
                nc.vector.tensor_copy(shift_hl[:, :, 0], shift[:, :]).then_inc(mchain, 1)
                dve.wait_ge(mchain, b * 4 + 4)
                nc.vector.tensor_tensor(shift_hl[:, :, 1], shift[:, :], shift_hl[:, :, 0], ALU.subtract).then_inc(shift_ok, 1)

            def add_context(t, c, half):
                j, n = c % NJ, nth(t, c) * 2 + half
                dve.wait_ge(outp_ok, n + 1)
                rd = rden[:, 2 * half:2 * half + 2]
                nc.vector.reciprocal(rd, outp[:, :, DEN]).then_inc(den_ok, 1)
                dve.wait_ge(den_ok, n + 1)
                for i in range(2):
                    tile = j * QT + 2 * half + i
                    nc.vector.scalar_tensor_tensor(out=resid[:, tile, :], in0=outp[:, i, 0:D],
                                                   scalar=rden[:, 2 * half + i:2 * half + i + 1], in1=resid[:, tile, :],
                                                   op0=ALU.mult, op1=ALU.add).then_inc(added, 1)

            latent_queries(2)
            queries(0, 0)
            latent_queries(3)
            for n in range(AHEAD):
                unit(0, 0, n, early[n])
                if n == 4:
                    queries(0, 1)
                if n == UNITS - 1:
                    dve.wait_ge(pe_w, 5)
                    nc.vector.tensor_tensor(u[:, :].rearrange("p (h t) -> p h t", h=HEADS),
                                            ctx_ps[:, 0:KT * HEADS].rearrange("p (t h) -> p h t", h=HEADS),
                                            uconst[:, :].unsqueeze(2).to_broadcast([P, HEADS, KT]), ALU.add).then_inc(u_ok, 1)
                    dve.wait_ge(u_ok, 2)
                if n == UNITS - 1:
                    shifts(0, 0)
            dve.wait_ge(pool_r, 1)

            def body(t, c):
                for s in range(STEPS):
                    if s == 5 and is_block(t, c + 1):
                        shifts(t, c + 1)
                    k = s + AHEAD
                    if is_block(t, c + k // UNITS):
                        unit(t, c, k)
                    if s not in POOL_STEPS:
                        dve.wait_ge(pf_ok, nstep(t, c, s) + 1)
                        if step_index(t, c, s) >= NPH:
                            wait_used(dve, t, c, s)
                        nc.vector.tensor_tensor(p_lo[s % NPH][:, :], p_f[s % NPF][:, :], p_hi[s % NPH][:, :],
                                                ALU.subtract).then_inc(plo_dve, 1)
                    if s == 2 and is_block(t, c + 2):
                        queries(t, c + 2)
                    if s == 0 and not is_first(t, c):
                        context(t, c - 1)
                    if s in (3, 4) and not is_first(t, c):
                        add_context(t, c - 1, s - 3)
                    if s == STEPS - 1 and is_last(t):
                        transposed(c - 1)
                    if s == 5 and is_last(t):
                        dve.wait_ge(added, nth(t, c) * QT)
                        statistics(c - 1)
                    if s == 6 and is_last(t):
                        normalise(c - 1)

            def context(t, c):
                dve.wait_ge(ctx_ok, nth(t, c) + 1)
                nc.vector.tensor_tensor(ctx_f[:, :], ctx_ps[0:R + 1, :], ctx_low[:, :], ALU.add).then_inc(ctxsum_ok, 1)

            def transposed(j):
                dve.wait_ge(x1T_ok, j + 1)
                nc.vector.tensor_tensor(x1_lo[:, chunk(j)], misc[:, :], x1_hi[:, chunk(j)], ALU.subtract).then_inc(x1lo_ok, 1)

            def statistics(n):
                j = n % NJ
                for q in range(j * QT, (j + 1) * QT):
                    nc.vector.bn_stats(stats[:, q, :], resid[:, q, :]).then_inc(ln, 1)
                variances(n)

            def variances(n):
                j = n % NJ
                dve.wait_ge(ln, n * LN_ALL + QT)
                for q in range(j * QT, (j + 1) * QT):
                    nc.vector.bn_aggr(mv[:, q, :], stats[:, q, :]).then_inc(ln, 1)

            def normalise(n):
                j = n % NJ
                dve.wait_ge(pool_ln, 2 * n + 2)
                for q in range(j * QT, (j + 1) * QT):
                    nc.vector.tensor_scalar(resid[:, q, :], resid[:, q, :], mv[:, q, 0:1], rstd[:, q:q + 1],
                                            ALU.subtract, ALU.mult).then_inc(ln, 1)

            def result(j, parts):
                for n in range(parts):
                    dve.wait_ge(down_ok, 2 * j + 2 * (n + 1) // parts)
                    dve.wait_ge(ln, (j + 1) * LN_ALL)
                    for w in range(2):
                        for half in range(n * 2 // parts, (n + 1) * 2 // parts):
                            tokens = resid[:, j * QT + 2 * half:j * QT + 2 * half + 2, :]
                            sums = (ctx_ps, misc)[half][:, :].rearrange("p (q n d) -> p q n d", q=2, n=2)[:, :, w, :]
                            if w:
                                dve.wait_ge(y_hi, 2 * j + half + 1)
                            nc.vector.tensor_tensor(tokens, sums, tokens, ALU.add).then_inc(y_ok if w else y_hi, 1)
                    dve.wait_ge(y_ok, 2 * j + 2 * (n + 1) // parts)
                    for q in range(j * QT + n * QT // parts, j * QT + (n + 1) * QT // parts):
                        nc.vector.bn_stats(stats[:, q, :], resid[:, q, :]).then_inc(ln, 1)
                variances(NJ + j)

            blocks(dve, body)
            context(HEADS - 1, NJ - 1)
            for j in range(NJ):
                for k in range(HT):
                    if (j, k) == LAST_IN:
                        transposed(NJ - 1)
                    dve.wait_ge(sil_ok, j * HT + k + 1)
                    dve.wait_ge(up_ok, j * HT + k + 1)
                    if j:
                        dve.wait_ge(hlo_ok, (j - 1) * HT + k + 1)
                    nc.vector.tensor_tensor(h_f[:, k, :], up_t(k), sil[:, k, :], ALU.mult).then_inc(h_ok, 1)
                    if (j, k) == (NJ - 1, HT - 1):
                        dve.wait_ge(hhi_ok, NJ * HT)
                        dve.wait_ge(down_ok, 2 * (j - 1))
                        nc.vector.tensor_tensor(h_lo[j % 2][:, k, :], h_f[:, k, :], h_hi[j % 2][:, k, :],
                                                ALU.subtract).then_inc(hlo_last, 1)
                    if k == NORM_AT and j:
                        normalise(NJ + j - 2)
                if j == 0:
                    for half in range(2):
                        add_context(HEADS - 1, NJ - 1, half)
                    dve.wait_ge(added, NB * QT)
                    statistics(NJ - 1)
                if j:
                    result(j - 1, 1)
            normalise(2 * NJ - 2)
            result(NJ - 1, 2)
            normalise(2 * NJ - 1)

        @block.tensor
        def _(pe):
            def warm(dst, count):
                for n in range(count):
                    nc.tensor.matmul(dst[:, 0:P], ones[:, :], ones[:, :], start=True, stop=True)

            pe.wait_ge(const, 1)
            warm(misc, WARM)

            def latent_queries(c):
                nc.tensor.matmul(mscore[:, (c % 2) * QB:(c % 2 + 1) * QB], wlat_sb[:, 0, :], xT_sb[:, chunk(c)],
                                 start=True, stop=True).then_inc(pe_c, 1)

            pe.wait_ge(in_k, 16)
            for c in range(NJ):
                if c == 2:
                    pe.wait_ge(in_q, 16)
                    for h in range(HEADS):
                        last = nc.tensor.matmul(misc[:, h * (R + 1):(h + 1) * (R + 1)],
                                                uq4_sb[:, h, :], ukb_sb[:, h, :],
                                                start=True, stop=True)
                    last.then_inc(pe_w, 1)
                    for h in range(HEADS):
                        nc.tensor.matmul(ctx_ps[0:R, h:h + 1], ukb_sb[:, h, 0:R], buq_sb[:, h:h + 1], start=True, stop=True)
                    pe.wait_ge(u_ok, 1)
                    pe.wait_ge(const, CONST_ALL)
                    nc.tensor.matmul(ctx_ps[:, HEADS:2 * HEADS], ones[:, :], ub[:, :], start=True, stop=True).then_inc(pe_w, 1)
                pe.wait_ge(in_t[c], 16)
                if c < 2:
                    latent_queries(c)
                nc.tensor.matmul(score[c // 2][:, (c % 2) * QB:(c % 2 + 1) * QB], wlat_sb[:, 1, :], xT_sb[:, chunk(c)],
                                 start=True, stop=True).then_inc(pe_k, 1)
            pe.wait_ge(dve_c, 2)
            for c in range(2, NJ):
                latent_queries(c)

            def project(t, c):
                if c % NJ == 0:
                    pe.wait_ge(wq_ok, head_of(t, c) * 2 + 2)
                nc.tensor.matmul(misc[:, :], wq_now[:, :], cq_hl[:, chunk(c % NJ)],
                                 start=True, stop=True).then_inc(proj_ok, 1)

            def half_unit(j, k, n, dst=mscore):
                qt = q_hl[j][:, (k // 2) * P:(k // 2 + 1) * P]
                keys = slice((k % 2) * HALF + n * QB, (k % 2) * HALF + (n + 1) * QB)
                o = dst[:, n * QB:(n + 1) * QB]
                nc.tensor.matmul(o, qt, k_hi2[:, keys], start=True, stop=False)
                nc.tensor.matmul(o, qt, k_lo2[:, keys], start=False, stop=True).then_inc(unit_ok, 1)

            def rows(t, c):
                pe.wait_ge(shift_ok, nth(t, c) + 1)
                for q in range(QT):
                    last = nc.tensor.matmul(misc[0:2, q * P:(q + 1) * P], shift_hl[:, q, :], ident_r[:, :],
                                            start=True, stop=True)
                last.then_inc(row_ok, 1)

            def scores(j, s):
                for a in range(2):
                    kt = slice((2 * s + a) * P, (2 * s + a + 1) * P)
                    o = score[s % 2][:, a * QB:(a + 1) * QB]
                    nc.tensor.matmul(o, k_hi2[:, kt], q_hl[j][:, :], start=True, stop=False)
                    last = nc.tensor.matmul(o, k_lo1[:, kt], q_hm[j][:, :], start=False, stop=True)
                last.then_inc(score_ok, 1)

            def contract(t, c, s):
                k = s % STEPS
                pe.wait_ge(phi_ok, nstep(t, c, s) + 1)
                for a in range(2):
                    last = nc.tensor.matmul(ctx_ps[:, :], vals[:, 2 * k + a, :], p_hi[k % NPH][:, a * QB:(a + 1) * QB],
                                            start=(k == 0 and a == 0), stop=False)
                last.then_inc(pvhi_ok, 1)

            def contract_lo(t, c, s):
                k = s % STEPS
                wait_lo(pe, t, c, s - 1)
                wait_lo(pe, t, c, s)
                for kk in (k - 1, k):
                    for a in range(2):
                        last = nc.tensor.matmul(ctx_ps[FEAT * a:FEAT * (a + 1), :], vals_b[:, 2 * kk + a, :],
                                                p_lo[kk % NPH][:, a * QB:(a + 1) * QB],
                                                start=False, stop=(kk == STEPS - 1))
                last.then_inc(pvlo_ok, 1)

            def project_context(t, c, half):
                hd = head_of(t, c)
                w_hi, w_lo = (w[:, hd, :] if isinstance(hd, int) else
                              w[:, bass.ds(hd, 1), :].rearrange("p a d -> p (a d)") for w in (wvo_hi, wvo_lo))
                for i in range(2):
                    q = slice((2 * half + i) * P, (2 * half + i + 1) * P)
                    o = outp[:, i, 0:OC]
                    nc.tensor.matmul(o, ctx_hl[:, q], w_hi, start=True, stop=False)
                    last = nc.tensor.matmul(o, ctx_hl[0:R + 1, q], w_lo[0:R + 1], start=False, stop=True)
                last.then_inc(outp_ok, 1)

            def values(n):
                for t in range(n * KT // 2, (n + 1) * KT // 2):
                    o = (t % (KT // 2)) * 2 * R
                    nc.tensor.matmul(ctx_ps[:, o:o + R], k_hi2[0:R, t * P:(t + 1) * P], ident_r[0:R, 0:R],
                                     start=True, stop=True)
                    last = nc.tensor.matmul(ctx_ps[:, o + R:o + 2 * R], k_lo2[0:R, t * P:(t + 1) * P], ident_r[0:R, 0:R],
                                            start=True, stop=True)
                last.then_inc(pe_w, 1)

            def output_weights(n):
                for h in range(HH):
                    last = nc.tensor.matmul(misc[0:CR, h * D:(h + 1) * D], uv2_sb[:, n * HH + h, :],
                                            wo_sb[:, n * HH + h, :], start=True, stop=True)
                last.then_inc(pe_w, 1)

            pe.wait_ge(dve_c, 1)
            project(0, 0)
            pe.wait_ge(act_w, 5)
            warm(ctx_ps, WARM_SPLIT)
            pe.wait_ge(qlo_ok, 1)
            pe.wait_ge(dve_k, NJ)
            for n in range(AHEAD):
                if n == UNITS:
                    pe.wait_ge(qlo_ok, 2)
                if early[n] is mscore:
                    pe.wait_ge(dve_c, NJ)
                for i in range(2):
                    if early_before(n) is not None:
                        pe.wait_ge(unit_max, 2 * early_before(n) + i + 1)
                    half_unit(n // UNITS, n % UNITS, i, early[n])
                if n == 0:
                    pe.wait_ge(act_w, 5)
                    values(0)
                if n == 2:
                    pe.wait_ge(dve_c, 2)
                    project(0, 1)
                if n == 3:
                    pe.wait_ge(act_w, 8)
                    values(1)
                if n == 5:
                    pe.wait_ge(dve_c, NJ)
                    pe.wait_ge(act_w, 11)
                    for t in range(KT):
                        last = nc.tensor.matmul(ctx_ps[:, t * HEADS:(t + 1) * HEADS], cq_hl[:, t * P:(t + 1) * P], uw[:, :],
                                                start=True, stop=True)
                    last.then_inc(pe_w, 1)
                if n == AHEAD - 2:
                    rows(0, 0)
            pe.wait_ge(row_in, 1)
            pe.wait_ge(lo1_ok, NJ)
            scores(0, 0)
            pe.wait_ge(u_ok, 2)

            def body(t, c):
                first = is_first(t, c)
                for s in range(STEPS):
                    k = s + AHEAD
                    if s == 2 and is_block(t, c + 2):
                        pe.wait_ge(row_in, nth(t, c) + 1)
                        project(t, c + 2)
                    if s == 6 and is_block(t, c + 1):
                        if first:
                            pe.wait_ge(act_w, ACT_W_ALL)
                        else:
                            pe.wait_ge(added, nth(t, c) * QT)
                        rows(t, c + 1)
                    if is_block(t, c + k // UNITS):
                        if k % UNITS == 0:
                            pe.wait_ge(qlo_ok, nth(t, c + k // UNITS) + 1)
                        for i in range(2):
                            pe.wait_ge(unit_max, nhalf(t, c, k, i) - 1)
                            half_unit((c + k // UNITS) % NJ, k % UNITS, i)
                    nxt = c + (s + 1) // STEPS
                    if is_block(t, nxt):
                        if s == STEPS - 1:
                            pe.wait_ge(row_in, nth(t, c + 1) + 1)
                        if first and s == 0:
                            pe.wait_ge(unit_max, 2 * AHEAD)
                        else:
                            pe.wait_ge(pf_ok, nstep(t, c, s))
                        scores(nxt % NJ, (s + 1) % STEPS)
                    if not (first and s == 0):
                        if s == 1 and not first:
                            pe.wait_ge(ctxsum_ok, nth(t, c))
                        cc = c - 1 if s == 0 else c
                        contract(t, cc, (s - 1) % STEPS)
                        if s in LO_AT:
                            contract_lo(t, cc, LO_AT[s])
                    if s == 3 and first:
                        pe.wait_ge(in_v, 16)
                        pe.wait_ge(qlo_ok, 3)
                        output_weights(0)
                    if s == 4 and first:
                        pe.wait_ge(act_w, ACT_W_ALL - 1)
                        output_weights(1)
                    if s in (3, 4) and not first:
                        if s == 3:
                            pe.wait_ge(ctxlo_ok, nth(t, c))
                            if first_use(t, c):
                                pe.wait_ge(wvo_ok, 2)
                            if is_last(t) and c >= 2:
                                pe.wait_ge(x1lo_ok, c - 1)
                            elif is_block(t, c + 2):
                                pe.wait_ge(qlo_ok, nth(t, c + 2) + 1)
                            else:
                                pe.wait_ge(row_in, nth(t, c) + 1)
                        else:
                            pe.wait_ge(added, nth(t, c - 1) * QT + 2)
                        project_context(t, c - 1, s - 3)
                    if s == STEPS - 1 and is_last(t):
                        if is_block(t, c + 1):
                            pe.wait_ge(row_in, nth(t, c) + 2)
                        transpose(c - 1)

            def transpose(j):
                pe.wait_ge(ln, (j + 1) * LN_ALL)
                for q in range(QT):
                    last = nc.tensor.transpose(misc[:, q * P:(q + 1) * P], resid[:, j * QT + q, :], ident[:, :])
                last.then_inc(x1T_ps, 1)

            blocks(pe, body)
            contract(HEADS - 1, NJ - 1, STEPS - 1)
            contract_lo(HEADS - 1, NJ - 1, STEPS - 1)
            pe.wait_ge(ffw_ok, 3)
            pe.wait_ge(pf_ok, NB * STEPS)

            def gate_up(j):
                pe.wait_ge(x1lo_ok, j + 1)
                for k in range(HT):
                    if (j, k) == LAST_IN:
                        pe.wait_ge(y_ok, 2)
                        transpose(NJ - 1)
                    if j:
                        pe.wait_ge(h_ok, (j - 1) * HT + k + 1)
                    for off, dst, done in ((0, gate_t(k), gate_ok), (H, up_t(k), up_ok)):
                        w = slice(off + k * P, off + (k + 1) * P)
                        nc.tensor.matmul(dst, wf_hi[:, w], x1_hi[:, chunk(j)], start=True, stop=False)
                        nc.tensor.matmul(dst, wf_lo[:, w], x1_hi[:, chunk(j)], start=False, stop=False)
                        nc.tensor.matmul(dst, wf_hi[:, w], x1_lo[:, chunk(j)], start=False, stop=True).then_inc(done, 1)

            def down(j):
                if j == NJ - 1:
                    pe.wait_ge(h_ok, j * HT + 1)
                    warm(score[0], WARM_HIDDEN)
                pe.wait_ge(hlo_ok, j * HT + HT - (j == NJ - 1))
                if j == NJ - 1:
                    pe.wait_ge(hlo_last, 1)
                if j == 0:
                    pe.wait_ge(added, NB * QT)
                else:
                    pe.wait_ge(y_ok, 2 * j)
                    pe.wait_ge(x1lo_ok, NJ)
                for q in range(QT):
                    tok = slice(q * P, (q + 1) * P)
                    o = down_t(q)
                    for k in range(HT):
                        w = slice(2 * H + k * D, 2 * H + (k + 1) * D)
                        if k < HT - 1:
                            nc.tensor.matmul(o, h_hi[j % 2][:, k, tok], wf_hl[:, :, w], start=(k == 0), stop=False)
                        last = nc.tensor.matmul(o[:, 0, :], h_lo[j % 2][:, k, tok], wf_hi[:, w], start=False, stop=False)
                        if k == HT - 1:
                            last = nc.tensor.matmul(o, h_hi[j % 2][:, k, tok], wf_hl[:, :, w], start=False, stop=True)
                    if q % 2 == 1:
                        last.then_inc(down_ok, 1)

            for j in range(NJ):
                gate_up(j)
                if j == 0:
                    pe.wait_ge(x1lo_ok, NJ - 1)
                    pe.wait_ge(ctxlo_ok, NB)
                    project_context(HEADS - 1, NJ - 1, 0)
                    pe.wait_ge(added, (NB - 1) * QT + 2)
                    project_context(HEADS - 1, NJ - 1, 1)
                if j:
                    down(j - 1)
            down(NJ - 1)


def kernel(**inputs):
    import concourse.bacc as bacc
    from concourse.bass_utils import run_bass_kernel_spmd

    a = {n.replace("L0_attn_", "").replace("L0_ffn_", ""): np.asarray(v) for n, v in inputs.items()}
    b, s, d = a["h_t"].shape
    r = a["W_DKV"].shape[1]
    heads = a["b_QR"].shape[0] // r
    dk = a["W_UK"].shape[1] // heads
    ht = a["w_down"].shape[1] // d

    def cat(*parts):
        return np.concatenate(parts, axis=-1)

    def by_head(w):
        return w.reshape(r, heads, dk).transpose(2, 1, 0)

    def bias(v):
        return v.reshape(heads, dk).T[:, :, None]

    x = a["h_t"].reshape(s, d)
    gap = np.zeros((r, heads), x.dtype)

    def load(*parts):
        return np.concatenate([p.reshape(p.shape[0], -1) for p in parts], axis=1)

    laid = {
        "x": x,
        "xT": x.T,
        "latw": load(cat(*[a["W_DQ"]] * 4), cat(a["W_DKV"], a["W_KR"], a["W_DKV"], a["W_KR"]),
                     cat(*[a["b_DQ"]] * 4)[:, None], cat(a["b_DKV"], a["b_KR"], a["b_DKV"], a["b_KR"])[:, None]),
        "qw": load(cat(*[by_head(a["W_UQ"])] * 4), cat(by_head(a["W_UK"]), bias(a["b_UK"])),
                   a["b_UQ"].reshape(heads, dk).T, np.concatenate([gap, a["b_QR"].reshape(heads, r).T] * 2)),
        "wqr4": np.concatenate([a["W_QR"].reshape(r, heads, r)] * 4),
        "vw": load(cat(by_head(a["W_UV"]), bias(a["b_UV"]), np.zeros((dk, heads, r - 1), x.dtype),
                       by_head(a["W_UV"]), bias(a["b_UV"])),
                   a["W_O"].reshape(heads, dk, d).transpose(1, 0, 2)),
        "bo": a["b_O"],
        "ffw": load(a["w_gate"].T, a["w_up"].T, a["w_down"].T.reshape(ht, d, d).transpose(1, 0, 2)),
    }
    nc = bacc.Bacc("TRN2", target_bir_lowering=False, num_devices=1)
    arrays, args = {}, []
    for n, v in laid.items():
        arrays[f"in_{n}"] = np.ascontiguousarray(v)
        args.append(nc.dram_tensor(f"in_{n}", v.shape, mybir.dt.from_np(v.dtype), kind="ExternalInput").ap())
    args.append(nc.dram_tensor("out_0", (s, d), F32, kind="ExternalOutput").ap())
    attention_ffn(nc, *args, HEADS=heads)
    res = run_bass_kernel_spmd(nc, [arrays], core_ids=[0])
    return res.results[0]["out_0"].reshape(b, s, d)
```
